# Optimizing a Trainium2 kernel written in Bass

```python
import numpy as np
import jax
import jax.numpy as jnp

def _softmax(x, axis=-1):
    return jax.nn.softmax(x, axis=axis)

def _gelu(x):
    return jax.nn.gelu(x, approximate=True)

def _silu(x):
    return jax.nn.silu(x)

def _sigmoid(x):
    return jax.nn.sigmoid(x)

def _layernorm(x, axis=-1, eps=1e-05):
    m = jnp.mean(x, axis=axis, keepdims=True)
    v = jnp.var(x, axis=axis, keepdims=True)
    return (x - m) / jnp.sqrt(v + eps)

def _scatter_add(tgt, idx, src, axis=0):
    return tgt.at[idx].add(src)

def _segment_sum(src, seg, n):
    return jax.ops.segment_sum(src, seg, n)
kernel_name = 'mk_sandwich_d2_jaxref_r8_06790c'

def setup_inputs(seed: int=0):
    np.random.seed(seed)
    _w = jnp.asarray

    def _L0_attn_setup():
        import jax, jax.numpy as jnp
        from jax import lax
        import numpy as np
        import math
        D_MODEL = 128
        D_STATE = 32
        D_CONV = 4
        EXPAND = 2
        D_INNER = EXPAND * D_MODEL
        DT_RANK = math.ceil(D_MODEL / 16)
        B, L = (4, 256)
        EPS = 1e-06

        def _rmsnorm(x, w):
            var = jnp.mean(x * x, axis=-1, keepdims=True)
            return x * lax.rsqrt(var + EPS) * w

        def _causal_depthwise_conv(x, conv_w, conv_b):
            xc = jnp.swapaxes(x, 1, 2)
            k = conv_w[:, None, :]
            y = lax.conv_general_dilated(xc, k, window_strides=(1,), padding=[(D_CONV - 1, 0)], dimension_numbers=('NCH', 'OIH', 'NCH'), feature_group_count=D_INNER)
            y = y + conv_b[None, :, None]
            return jnp.swapaxes(y, 1, 2)

        def _selective_scan(u, dt, A, Bm, Cm, D):

            def step(h, inp):
                ut, dtt, Bt, Ct = inp
                dA = jnp.exp(dtt[..., None] * A)
                h = dA * h + dtt[..., None] * Bt[:, None, :] * ut[..., None]
                y = jnp.einsum('bdn,bn->bd', h, Ct)
                return (h, y)
            h0 = jnp.zeros((u.shape[0], D_INNER, D_STATE), u.dtype)
            xs = (jnp.swapaxes(u, 0, 1), jnp.swapaxes(dt, 0, 1), jnp.swapaxes(Bm, 0, 1), jnp.swapaxes(Cm, 0, 1))
            _, ys = lax.scan(step, h0, xs)
            return jnp.swapaxes(ys, 0, 1) + u * D
        key = jax.random.key(seed)
        ks = jax.random.split(key, 10)
        x = jax.random.normal(ks[0], (B, L, D_MODEL), jnp.float32)
        norm_w = jnp.ones((D_MODEL,), jnp.float32)
        in_proj_w = jax.random.normal(ks[1], (2 * D_INNER, D_MODEL), jnp.float32) * 0.02
        conv_w = jax.random.normal(ks[2], (D_INNER, D_CONV), jnp.float32) * 0.1
        conv_b = jnp.zeros((D_INNER,), jnp.float32)
        x_proj_w = jax.random.normal(ks[3], (DT_RANK + 2 * D_STATE, D_INNER), jnp.float32) * 0.02
        dt_proj_w = jax.random.normal(ks[4], (D_INNER, DT_RANK), jnp.float32) * DT_RANK ** (-0.5)
        dt = jnp.exp(jax.random.uniform(ks[5], (D_INNER,)) * (np.log(0.1) - np.log(0.001)) + np.log(0.001))
        dt_proj_b = dt + jnp.log(-jnp.expm1(-dt))
        A_log = jnp.log(jnp.tile(jnp.arange(1, D_STATE + 1, dtype=jnp.float32)[None, :], (D_INNER, 1)))
        D_param = jnp.ones((D_INNER,), jnp.float32)
        out_proj_w = jax.random.normal(ks[6], (D_MODEL, D_INNER), jnp.float32) * 0.02
        return {'x': x, 'norm_w': norm_w, 'in_proj_w': in_proj_w, 'conv_w': conv_w, 'conv_b': conv_b, 'x_proj_w': x_proj_w, 'dt_proj_w': dt_proj_w, 'dt_proj_b': dt_proj_b, 'A_log': A_log, 'D_param': D_param, 'out_proj_w': out_proj_w}
    _L0_attn_in = _L0_attn_setup()

    def _L0_ffn_setup():
        import jax, jax.numpy as jnp
        import numpy as np
        D_IN, D_HID = (128, 512)

        def _ternary(key, shape):
            return jax.random.randint(key, shape, -1, 2).astype(jnp.float32)

        def _tlin(x, w, s):
            return jnp.einsum('bsi,oi->bso', x, w) * s
        key = jax.random.key(seed)
        ks = jax.random.split(key, 12)
        inv = lambda fan: 1.0 / np.sqrt(fan).astype(np.float32)
        return {'x': jax.random.normal(ks[0], (4, 256, D_IN), dtype=jnp.float32), 'w1_w': _ternary(ks[1], (D_HID, D_IN)), 'w1_s': jax.random.uniform(ks[2], (D_HID,), dtype=jnp.float32) * inv(D_IN), 'w2_w': _ternary(ks[3], (D_HID, D_IN)), 'w2_s': jax.random.uniform(ks[4], (D_HID,), dtype=jnp.float32) * inv(D_IN), 'h1_w': _ternary(ks[5], (D_HID, D_HID)), 'h1_s': jax.random.uniform(ks[6], (D_HID,), dtype=jnp.float32) * inv(D_HID), 'h2_w': _ternary(ks[7], (D_HID, D_HID)), 'h2_s': jax.random.uniform(ks[8], (D_HID,), dtype=jnp.float32) * inv(D_HID), 'w3_w': _ternary(ks[9], (D_IN, D_HID)), 'w3_s': jax.random.uniform(ks[10], (D_IN,), dtype=jnp.float32) * inv(D_HID)}
    _L0_ffn_in = _L0_ffn_setup()

    def _L1_attn_setup():
        import jax, jax.numpy as jnp
        import numpy as np
        B, N, E, H, DEPTH = (2, 256, 128, 8, 12)
        D = E // H // 2
        LN_EPS = 1e-05
        key = jax.random.key(seed)
        ks = jax.random.split(key, 10)
        w = lambda k: jax.random.normal(k, (E, E), jnp.float32) * E ** (-0.5)
        lp = lambda k: jax.random.normal(k, (D,), jnp.float32) * 0.1
        return {'x': jax.random.normal(ks[0], (B, N, E), jnp.float32), 'Wq': w(ks[1]), 'Wk': w(ks[2]), 'Wv': w(ks[3]), 'Wo': w(ks[4]), 'lq1': lp(ks[5]), 'lk1': lp(ks[6]), 'lq2': lp(ks[7]), 'lk2': lp(ks[8]), 'ln_g': jnp.ones((2 * D,), jnp.float32), 'ln_b': jnp.zeros((2 * D,), jnp.float32)}
    _L1_attn_in = _L1_attn_setup()

    def _L1_ffn_setup():
        import jax, jax.numpy as jnp
        import numpy as np
        from jax import lax
        B, S, H = (2, 128, 128)
        I = 64
        E = 32
        TOP_K = 4
        N_GROUP = 4
        TOPK_GROUP = 2
        SCALE = 2.5
        N_SHARED = 2
        SH_I = I * N_SHARED

        def _route(tokens, router_weight, router_bias):
            logits = tokens.astype(jnp.float32) @ router_weight.astype(jnp.float32).T
            scores = jax.nn.sigmoid(logits)
            sfc = scores + router_bias[None, :]
            T = tokens.shape[0]
            grp = sfc.reshape(T, N_GROUP, E // N_GROUP)
            group_scores = lax.top_k(grp, 2)[0].sum(-1)
            _, gidx = lax.top_k(group_scores, TOPK_GROUP)
            gmask = jax.nn.one_hot(gidx, N_GROUP, dtype=sfc.dtype).sum(1)
            smask = jnp.broadcast_to(gmask[:, :, None], (T, N_GROUP, E // N_GROUP)).reshape(T, E)
            tmp = jnp.where(smask > 0, sfc, 0.0)
            _, topk_idx = lax.top_k(tmp, TOP_K)
            topk_w = jnp.take_along_axis(scores, topk_idx, axis=1)
            topk_w = topk_w / (topk_w.sum(-1, keepdims=True) + 1e-20)
            topk_w = topk_w * SCALE
            return (topk_idx, topk_w)
        key = jax.random.key(seed)
        ks = jax.random.split(key, 10)
        std = 0.02
        return {'hidden_states': jax.random.normal(ks[0], (B, S, H), jnp.float32), 'router_weight': jax.random.normal(ks[1], (E, H), jnp.float32) * std, 'router_bias': jnp.zeros((E,), jnp.float32), 'gate_w': jax.random.normal(ks[2], (E, I, H), jnp.float32) * std, 'up_w': jax.random.normal(ks[3], (E, I, H), jnp.float32) * std, 'down_w': jax.random.normal(ks[4], (E, H, I), jnp.float32) * std, 'shared_gate_w': jax.random.normal(ks[5], (SH_I, H), jnp.float32) * std, 'shared_up_w': jax.random.normal(ks[6], (SH_I, H), jnp.float32) * std, 'shared_down_w': jax.random.normal(ks[7], (H, SH_I), jnp.float32) * std}
    _L1_ffn_in = _L1_ffn_setup()
    _d = {'L0_attn_x': _L0_attn_in['x'], 'L0_attn_norm_w': _L0_attn_in['norm_w'], 'L0_attn_in_proj_w': _L0_attn_in['in_proj_w'], 'L0_attn_conv_w': _L0_attn_in['conv_w'], 'L0_attn_conv_b': _L0_attn_in['conv_b'], 'L0_attn_x_proj_w': _L0_attn_in['x_proj_w'], 'L0_attn_dt_proj_w': _L0_attn_in['dt_proj_w'], 'L0_attn_dt_proj_b': _L0_attn_in['dt_proj_b'], 'L0_attn_A_log': _L0_attn_in['A_log'], 'L0_attn_D_param': _L0_attn_in['D_param'], 'L0_attn_out_proj_w': _L0_attn_in['out_proj_w'], 'L0_ffn_w1_w': _L0_ffn_in['w1_w'], 'L0_ffn_w1_s': _L0_ffn_in['w1_s'], 'L0_ffn_w2_w': _L0_ffn_in['w2_w'], 'L0_ffn_w2_s': _L0_ffn_in['w2_s'], 'L0_ffn_h1_w': _L0_ffn_in['h1_w'], 'L0_ffn_h1_s': _L0_ffn_in['h1_s'], 'L0_ffn_h2_w': _L0_ffn_in['h2_w'], 'L0_ffn_h2_s': _L0_ffn_in['h2_s'], 'L0_ffn_w3_w': _L0_ffn_in['w3_w'], 'L0_ffn_w3_s': _L0_ffn_in['w3_s'], 'L1_attn_Wq': _L1_attn_in['Wq'], 'L1_attn_Wk': _L1_attn_in['Wk'], 'L1_attn_Wv': _L1_attn_in['Wv'], 'L1_attn_Wo': _L1_attn_in['Wo'], 'L1_attn_lq1': _L1_attn_in['lq1'], 'L1_attn_lk1': _L1_attn_in['lk1'], 'L1_attn_lq2': _L1_attn_in['lq2'], 'L1_attn_lk2': _L1_attn_in['lk2'], 'L1_attn_ln_g': _L1_attn_in['ln_g'], 'L1_attn_ln_b': _L1_attn_in['ln_b'], 'L1_ffn_router_weight': _L1_ffn_in['router_weight'], 'L1_ffn_router_bias': _L1_ffn_in['router_bias'], 'L1_ffn_gate_w': _L1_ffn_in['gate_w'], 'L1_ffn_up_w': _L1_ffn_in['up_w'], 'L1_ffn_down_w': _L1_ffn_in['down_w'], 'L1_ffn_shared_gate_w': _L1_ffn_in['shared_gate_w'], 'L1_ffn_shared_up_w': _L1_ffn_in['shared_up_w'], 'L1_ffn_shared_down_w': _L1_ffn_in['shared_down_w']}
    _x0 = _d['L0_attn_x']
    _d['L0_attn_x'] = jax.random.normal(jax.random.fold_in(jax.random.key(seed), 1), (16, 512, 128), dtype=_x0.dtype)
    del _x0
    return _d

def reference(L0_attn_x, L0_attn_norm_w, L0_attn_in_proj_w, L0_attn_conv_w, L0_attn_conv_b, L0_attn_x_proj_w, L0_attn_dt_proj_w, L0_attn_dt_proj_b, L0_attn_A_log, L0_attn_D_param, L0_attn_out_proj_w, L0_ffn_w1_w, L0_ffn_w1_s, L0_ffn_w2_w, L0_ffn_w2_s, L0_ffn_h1_w, L0_ffn_h1_s, L0_ffn_h2_w, L0_ffn_h2_s, L0_ffn_w3_w, L0_ffn_w3_s, L1_attn_Wq, L1_attn_Wk, L1_attn_Wv, L1_attn_Wo, L1_attn_lq1, L1_attn_lk1, L1_attn_lq2, L1_attn_lk2, L1_attn_ln_g, L1_attn_ln_b, L1_ffn_router_weight, L1_ffn_router_bias, L1_ffn_gate_w, L1_ffn_up_w, L1_ffn_down_w, L1_ffn_shared_gate_w, L1_ffn_shared_up_w, L1_ffn_shared_down_w):

    def _L0_attn_ref(x, norm_w, in_proj_w, conv_w, conv_b, x_proj_w, dt_proj_w, dt_proj_b, A_log, D_param, out_proj_w):
        import jax, jax.numpy as jnp
        from jax import lax
        import numpy as np
        import math
        D_MODEL = 128
        D_STATE = 32
        D_CONV = 4
        EXPAND = 2
        D_INNER = EXPAND * D_MODEL
        DT_RANK = math.ceil(D_MODEL / 16)
        B, L = (4, 256)
        EPS = 1e-06

        def _rmsnorm(x, w):
            var = jnp.mean(x * x, axis=-1, keepdims=True)
            return x * lax.rsqrt(var + EPS) * w

        def _causal_depthwise_conv(x, conv_w, conv_b):
            xc = jnp.swapaxes(x, 1, 2)
            k = conv_w[:, None, :]
            y = lax.conv_general_dilated(xc, k, window_strides=(1,), padding=[(D_CONV - 1, 0)], dimension_numbers=('NCH', 'OIH', 'NCH'), feature_group_count=D_INNER)
            y = y + conv_b[None, :, None]
            return jnp.swapaxes(y, 1, 2)

        def _selective_scan(u, dt, A, Bm, Cm, D):

            def step(h, inp):
                ut, dtt, Bt, Ct = inp
                dA = jnp.exp(dtt[..., None] * A)
                h = dA * h + dtt[..., None] * Bt[:, None, :] * ut[..., None]
                y = jnp.einsum('bdn,bn->bd', h, Ct)
                return (h, y)
            h0 = jnp.zeros((u.shape[0], D_INNER, D_STATE), u.dtype)
            xs = (jnp.swapaxes(u, 0, 1), jnp.swapaxes(dt, 0, 1), jnp.swapaxes(Bm, 0, 1), jnp.swapaxes(Cm, 0, 1))
            _, ys = lax.scan(step, h0, xs)
            return jnp.swapaxes(ys, 0, 1) + u * D
        xn = _rmsnorm(x, norm_w)
        xz = jnp.einsum('bld,ed->ble', xn, in_proj_w)
        u, z = jnp.split(xz, 2, axis=-1)
        u = jax.nn.silu(_causal_depthwise_conv(u, conv_w, conv_b))
        dbl = jnp.einsum('bld,ed->ble', u, x_proj_w)
        dt, Bm, Cm = jnp.split(dbl, [DT_RANK, DT_RANK + D_STATE], axis=-1)
        dt = jax.nn.softplus(jnp.einsum('blr,dr->bld', dt, dt_proj_w) + dt_proj_b)
        A = -jnp.exp(A_log)
        y = _selective_scan(u, dt, A, Bm, Cm, D_param)
        y = y * jax.nn.silu(z)
        out = jnp.einsum('ble,de->bld', y, out_proj_w)
        return x + out

    def _L0_ffn_ref(x, w1_w, w1_s, w2_w, w2_s, h1_w, h1_s, h2_w, h2_s, w3_w, w3_s):
        import jax, jax.numpy as jnp
        import numpy as np
        D_IN, D_HID = (128, 512)

        def _ternary(key, shape):
            return jax.random.randint(key, shape, -1, 2).astype(jnp.float32)

        def _tlin(x, w, s):
            return jnp.einsum('bsi,oi->bso', x, w) * s
        h = jax.nn.silu(_tlin(x, w1_w, w1_s)) * _tlin(x, w2_w, w2_s)
        h = jax.nn.gelu(_tlin(h, h1_w, h1_s), approximate=False)
        h = jax.nn.gelu(_tlin(h, h2_w, h2_s), approximate=False)
        return _tlin(h, w3_w, w3_s)

    def _L1_attn_ref(x, Wq, Wk, Wv, Wo, lq1, lk1, lq2, lk2, ln_g, ln_b):
        import jax, jax.numpy as jnp
        import numpy as np
        B, N, E, H, DEPTH = (2, 256, 128, 8, 12)
        D = E // H // 2
        LN_EPS = 1e-05
        b, n, e = x.shape
        lam_init = 0.8 - 0.6 * np.exp(-0.3 * DEPTH)
        q = (x @ Wq).reshape(b, n, 2 * H, D).transpose(0, 2, 1, 3) * D ** (-0.5)
        k = (x @ Wk).reshape(b, n, 2 * H, D).transpose(0, 2, 1, 3)
        v = (x @ Wv).reshape(b, n, H, 2 * D).transpose(0, 2, 1, 3)
        scores = jnp.einsum('bhqd,bhkd->bhqk', q, k)
        attn = jax.nn.softmax(scores, axis=-1).reshape(b, H, 2, n, n)
        lam = jnp.exp(jnp.sum(lq1 * lk1)) - jnp.exp(jnp.sum(lq2 * lk2)) + lam_init
        w_diff = attn[:, :, 0] - lam * attn[:, :, 1]
        o = jnp.einsum('bhqk,bhkd->bhqd', w_diff, v)
        mu = o.mean(-1, keepdims=True)
        var = ((o - mu) ** 2).mean(-1, keepdims=True)
        o = (o - mu) * jax.lax.rsqrt(var + LN_EPS) * ln_g + ln_b
        o = o.transpose(0, 2, 1, 3).reshape(b, n, e)
        return o @ Wo

    def _L1_ffn_ref(hidden_states, router_weight, router_bias, gate_w, up_w, down_w, shared_gate_w, shared_up_w, shared_down_w):
        import jax, jax.numpy as jnp
        import numpy as np
        from jax import lax
        B, S, H = (2, 128, 128)
        I = 64
        E = 32
        TOP_K = 4
        N_GROUP = 4
        TOPK_GROUP = 2
        SCALE = 2.5
        N_SHARED = 2
        SH_I = I * N_SHARED

        def _route(tokens, router_weight, router_bias):
            logits = tokens.astype(jnp.float32) @ router_weight.astype(jnp.float32).T
            scores = jax.nn.sigmoid(logits)
            sfc = scores + router_bias[None, :]
            T = tokens.shape[0]
            grp = sfc.reshape(T, N_GROUP, E // N_GROUP)
            group_scores = lax.top_k(grp, 2)[0].sum(-1)
            _, gidx = lax.top_k(group_scores, TOPK_GROUP)
            gmask = jax.nn.one_hot(gidx, N_GROUP, dtype=sfc.dtype).sum(1)
            smask = jnp.broadcast_to(gmask[:, :, None], (T, N_GROUP, E // N_GROUP)).reshape(T, E)
            tmp = jnp.where(smask > 0, sfc, 0.0)
            _, topk_idx = lax.top_k(tmp, TOP_K)
            topk_w = jnp.take_along_axis(scores, topk_idx, axis=1)
            topk_w = topk_w / (topk_w.sum(-1, keepdims=True) + 1e-20)
            topk_w = topk_w * SCALE
            return (topk_idx, topk_w)
        tokens = hidden_states.reshape(-1, H)
        topk_idx, topk_w = _route(tokens, router_weight, router_bias)
        gate_vals = jax.nn.silu(jnp.einsum('th,eih->tei', tokens, gate_w))
        up_vals = jnp.einsum('th,eih->tei', tokens, up_w)
        hidden_vals = gate_vals * up_vals
        expert_out = jnp.einsum('tei,ehi->teh', hidden_vals, down_w)
        sel = jnp.take_along_axis(expert_out, topk_idx[:, :, None], axis=1)
        mixed = (sel * topk_w[:, :, None].astype(sel.dtype)).sum(1)
        mixed = mixed.reshape(hidden_states.shape)
        sg = jax.nn.silu(jnp.einsum('bsh,ih->bsi', hidden_states, shared_gate_w))
        su = jnp.einsum('bsh,ih->bsi', hidden_states, shared_up_w)
        shared = jnp.einsum('bsi,hi->bsh', sg * su, shared_down_w)
        return mixed + shared
    x = L0_attn_x
    x = x + _layernorm(_L0_attn_ref(_layernorm(x, axis=-1), L0_attn_norm_w, L0_attn_in_proj_w, L0_attn_conv_w, L0_attn_conv_b, L0_attn_x_proj_w, L0_attn_dt_proj_w, L0_attn_dt_proj_b, L0_attn_A_log, L0_attn_D_param, L0_attn_out_proj_w), axis=-1)
    x = x + _layernorm(_L0_ffn_ref(_layernorm(x, axis=-1), L0_ffn_w1_w, L0_ffn_w1_s, L0_ffn_w2_w, L0_ffn_w2_s, L0_ffn_h1_w, L0_ffn_h1_s, L0_ffn_h2_w, L0_ffn_h2_s, L0_ffn_w3_w, L0_ffn_w3_s), axis=-1)
    x = x + _layernorm(_L1_attn_ref(_layernorm(x, axis=-1), L1_attn_Wq, L1_attn_Wk, L1_attn_Wv, L1_attn_Wo, L1_attn_lq1, L1_attn_lk1, L1_attn_lq2, L1_attn_lk2, L1_attn_ln_g, L1_attn_ln_b), axis=-1)
    x = x + _layernorm(_L1_ffn_ref(_layernorm(x, axis=-1), L1_ffn_router_weight, L1_ffn_router_bias, L1_ffn_gate_w, L1_ffn_up_w, L1_ffn_down_w, L1_ffn_shared_gate_w, L1_ffn_shared_up_w, L1_ffn_shared_down_w), axis=-1)
    return x

_drawn_inputs = setup_inputs


def setup_inputs(seed=0):
    import zlib

    import numpy as np

    out = dict(_drawn_inputs(seed))
    spreads = {'L0_attn_norm_w': (1.0, 0.6),
     'L0_attn_conv_b': (0.0, 0.8),
     'L0_attn_D_param': (1.0, 0.6),
     'L1_attn_ln_g': (1.0, 0.2),
     'L1_attn_ln_b': (0.0, 0.1),
     'L1_ffn_router_bias': (0.0, 0.1)}
    factors = {'L0_attn_in_proj_w': 6.824,
     'L0_attn_conv_w': 8.0,
     'L0_attn_x_proj_w': 8.0,
     'L0_attn_dt_proj_w': 8.0,
     'L0_attn_dt_proj_b': 8.0,
     'L0_attn_A_log': 8.0,
     'L0_attn_out_proj_w': 7.655,
     'L1_attn_lq1': 4.078,
     'L1_attn_lk1': 2.895}
    for name, (base, spread) in spreads.items():
        noise = np.random.default_rng([zlib.crc32(name.encode()), seed]).standard_normal(out[name].shape)
        drawn = base * np.exp(spread * noise) if base else spread * noise
        out[name] = jnp.asarray(drawn.astype(out[name].dtype))
    for name, factor in factors.items():
        out[name] = (out[name] * factor).astype(out[name].dtype)
    return out
```

```python
from contextlib import ExitStack

import numpy as np

import concourse.bass as bass
from concourse import mybir

F32 = mybir.dt.float32
BF16 = mybir.dt.bfloat16
ALU = mybir.AluOpType
ACT = mybir.ActivationFunctionType
AX = mybir.AxisListType

P = 128
D = 128
T = 512
TJ = T // P
LN_EPS = 1e-5
RMS_EPS = 1e-6
LEAD = 3

NS = 32
DI = 256
NH = DI // P
TAPS = 4
RANK = 8
DG = P // NS
NT = DI // DG
QR = 4
PARTS = 3
JT = 32 // DG
HT = NT // NH

FH = 512
FK = FH // P


class Signal:

    def __init__(self, sem, per, lead=LEAD):
        self.sem, self.per, self.lead = sem, per, lead

    def at(self, step, k=None):
        return (step + self.lead) * self.per + (self.per if k is None else k)


def columns(parts):
    at, out = 0, {}
    for name, width in parts:
        out[name] = (at, width)
        at += width
    return out, at


W0_PARTS = [
    ("ident", P), ("norm_w", 1), ("conv_b", NH), ("dt_b", NH), ("d_skip", NH), ("a_log", NT),
    ("xb_w", NH * P), ("xc_w", NH * P), ("xr_w", NH * RANK),
    ("dt_w", DI), ("out_w", NH * D), ("gather", JT * 32),
    ("w1_s", FK), ("w2_s", FK), ("h1_s", FK), ("h2_s", FK), ("w3_s", D),
    ("w1", FH), ("w2", FH), ("h1", FK * FH), ("h2", FK * FH), ("w3", FK * D),
]
S0_PARTS = [("in_w", 2 * DI), ("conv_w", TAPS * DI), ("spread", JT * P)]
W0_COLS, W0_WIDTH = columns(W0_PARTS)
S0_COLS, S0_WIDTH = columns(S0_PARTS)


FRONT = 2


def layer0(nc, ctx, sems, passed, x_in, w0_in, s0_in, xr, out, NB):

    def sb(name, shape, dtype=F32):
        return ctx.enter_context(nc.sbuf_tensor(name, shape, dtype))

    def pb(name, shape):
        return ctx.enter_context(nc.psum_tensor(name, shape, F32))

    def sem(name):
        return sems.enter_context(nc.semaphore(name))

    signals = {e: [] for e in ("vector", "scalar", "tensor", "gpsimd", "sync")}

    def signal(engine, name, per=1, early=0):
        s = Signal(sem(name), per)
        s.start = LEAD * per - early
        signals[engine].append(s)
        return s

    def prime(eng, engine):
        for s in signals[engine]:
            eng.sem_inc(s.sem, s.start)

    w = sb("w0", [P, W0_WIDTH])

    def W(name, *shape):
        a, n = W0_COLS[name]
        v = w[:, a:a + n]
        if len(shape) == 2:
            v = v.rearrange("p (a b) -> p a b", a=shape[0])
        return v

    def S(name, *shape):
        a, n = S0_COLS[name]
        v = setup_area[:, a:a + n]
        return v.rearrange("p (a b) -> p a b", a=shape[0]) if len(shape) == 2 else v

    ident = W("ident")
    gather = W("gather", JT, 32)

    half_neg = sb("minus_half", [P, TJ])
    a_neg = sb("a_neg", [P, NT])
    w_taps = sb("w_taps", [P, TAPS, DI])
    w_z = sb("w_z", [P, DI])

    st = sb("ln_stats", [P, 4, TJ, 6])
    mv = sb("ln_mean_var", [P, 4, TJ, 2])
    rs = sb("ln_rstd", [P, 4, TJ])
    tmp = sb("rms_tmp", [P, TJ])
    s2 = sb("rms_scale", [P, TJ])
    h = sb("mix_in", [P, 2, TJ, D])
    rn = sb("rms_normed", [P, TJ, D])
    rnT = sb("rms_normed_T", [P, TAPS - 1 + T])
    u = sb("u", [P, 2, NH, T])
    z = sb("z", [P, 2, NH, T])
    dtr = sb("dt_rank", [RANK, T])
    brep = sb("b_rep", [P, 2, T])
    crep = sb("c_rep", [P, 2, T])
    dd = sb("dt_dtu", [P, 2, NH, T])
    parts = sb("dt_parts", [P, PARTS, 2 * NH, T], BF16)
    stack = sb("dt_stack", [PARTS * 32, QR, NH, 2, T], BF16)
    spread_b = sb("spread_b", [PARTS * 32, JT, P], BF16)
    setup_area = parts[:, :, :, :].rearrange("p k a t -> p (k a t)").bitcast(F32)
    ab, ex, kept = (parts[:, k, :, :].rearrange("p a t -> p (a t)").bitcast(F32)
                    .rearrange("p (a t) -> p a t", a=NH) for k in range(3))
    AHEAD = 2
    LATER = 2
    RA, RB, RH, RC = 4, 4, 4, 8
    dA = sb("decay", [P, RA, T])
    dB = sb("drive", [P, RB, T])
    hs = sb("state", [P, RH, T])
    hc = sb("state_c", [P, RC, T])
    mo = fo = sb("layer_out", [P, TJ, D])

    fx = rn
    fxT = sb("ffn_in_T", [P, T])
    fr = sb("ffn_raw", [P, FK, T])
    fg = sb("ffn_gated", [P, FK, T])

    p_dt = [pb(f"p_dt{k}", [P, T]) for k in range(2)]
    p_du = [pb(f"p_du{k}", [P, T]) for k in range(2)]
    p_y = pb("p_y", [P, T])
    p_a = pb("p_pre", [P, T])
    p_f = [pb(f"p_ffn{k}", [P, T]) for k in range(2)]

    loaded = sem("loaded")
    x_loaded = sem("x_loaded")
    setup_act = sem("setup_act")
    setup_vec = sem("setup_vec")
    setup_pool = sem("setup_pool")
    setup_pe = sem("setup_pe")

    dt_spread = signal("tensor", "dt_spread", NT)
    du_spread = signal("tensor", "du_spread", NT)
    decayed = signal("scalar", "decayed", NT)
    driven = signal("vector", "driven", NT)
    scanned = signal("vector", "scanned", NT)
    weighed = signal("gpsimd", "weighed", NT)
    gathered = signal("tensor", "gathered", NT // QR, 1)
    y_read = signal("vector", "y_read", NH, 1)
    y_done = signal("vector", "y_done", NH, 1)
    out_done = signal("tensor", "out_done", 1, 1)
    mo_read = signal("vector", "mo_read", 1, 1)
    mo_stats = signal("vector", "mo_stats", 1, 1)
    mo_rstd = signal("gpsimd", "mo_rstd", 1, 1)
    mo_added = signal("vector", "mo_added", 1, 1)
    a_stats = signal("vector", "a_stats")
    a_rstd = signal("gpsimd", "a_rstd")
    a_norm = signal("vector", "a_norm")
    h_norm = signal("vector", "h_norm")
    a_turned = signal("tensor", "a_turned")
    a_copied = signal("scalar", "a_copied")
    uz_ready = signal("tensor", "uz_ready", 4)
    uz_read = signal("scalar", "uz_read", 4)
    u_silu = signal("scalar", "u_silu")
    z_silu = signal("scalar", "z_silu")
    x_ready = signal("tensor", "x_ready", 3)
    x_read = signal("scalar", "x_read", 3)
    dtp_ready = signal("tensor", "dtp_ready", NH)
    dtp_read = signal("scalar", "dtp_read", NH)
    sp_abs = signal("scalar", "sp_abs")
    sp_exp = signal("scalar", "sp_exp")
    sp_ln = signal("scalar", "sp_ln")
    sp_kept = signal("vector", "sp_kept", 2)
    sp_rest = signal("gpsimd", "sp_rest", 2 * NH)
    dt_done = signal("vector", "dt_done", 3)
    part1 = signal("scalar", "part1")
    rest1 = signal("vector", "rest1")
    part2 = signal("scalar", "part2")
    part3 = signal("vector", "part3")
    stacked = [signal("sync", f"stacked{hh}", 16 * PARTS * QR) for hh in range(NH)]
    f_stats = signal("vector", "f_stats", 1, 1)
    f_rstd = signal("gpsimd", "f_rstd", 1, 1)
    f_norm = signal("vector", "f_norm", 1, 1)
    f_turned = signal("tensor", "f_turned", 1, 1)
    f_copied = signal("scalar", "f_copied", 1, 1)
    f1_ready = signal("tensor", "f1_ready", FK, FK)
    f1_read = signal("scalar", "f1_read", FK, FK)
    f_silu = signal("scalar", "f_silu", 1, 1)
    f2_ready = signal("tensor", "f2_ready", FK, FK)
    f_gated = signal("vector", "f_gated", FK, FK)
    g1_ready = signal("tensor", "g1_ready", FK, FK)
    g1_read = signal("scalar", "g1_read", FK, FK)
    g1_gelu = signal("scalar", "g1_gelu", 1, 1)
    g2_ready = signal("tensor", "g2_ready", FK, FK)
    g2_read = signal("scalar", "g2_read", FK, FK)
    g2_gelu = signal("scalar", "g2_gelu", 1, 1)
    f3_ready = signal("tensor", "f3_ready", 1, 2)
    f3_read = signal("vector", "f3_read", 1, 2)
    fo_stats = signal("vector", "fo_stats", 1, 2)
    fo_rstd = signal("gpsimd", "fo_rstd", 1, 2)
    fo_added = signal("vector", "fo_added", 1, 2)
    mo_bn = signal("vector", "mo_bn", 1, 1)
    mo_norm = signal("vector", "mo_norm", 1, 1)
    a_bn = signal("vector", "a_bn")
    f_bn = signal("vector", "f_bn", 1, 1)
    fo_bn = signal("vector", "fo_bn", 1, 2)
    fo_norm = signal("vector", "fo_norm", 1, 2)
    mo_var = signal("gpsimd", "mo_var", 1, 1)
    a_var = signal("gpsimd", "a_var", 6)
    f_var = signal("gpsimd", "f_var", 1, 1)
    fo_var = signal("gpsimd", "fo_var", 1, 2)

    SETUP_DMAS = 3

    def hold(eng):
        eng.sem_inc(passed, 1)

    def X(s):
        return xr[:, bass.ds((s + FRONT) * TJ, TJ), :]

    def Xj(s, j):
        return xr[:, bass.ds((s + FRONT) * TJ + j, 1), :].rearrange("p a d -> p (a d)")

    def tile(s, b, i):
        return (s, b, i) if i < NT else (s + 1, 1 - b, i - NT)

    block = ctx.enter_context(nc.Block())

    @block.sync
    def _(sp):
        x_tiles = x_in.rearrange("b (j p) d -> p (b j) d", p=P)
        sp.dma_start(xr[:, FRONT * TJ:(FRONT + 1) * TJ, :], x_tiles[:, 0:TJ, :]).then_inc(loaded, 16)
        sp.dma_start(setup_area[:, 0:S0_WIDTH], s0_in).then_inc(loaded, 16)
        sp.dma_start(w[:, :], w0_in).then_inc(loaded, 16)
        sp.dma_start(xr[:, (FRONT + 1) * TJ:(FRONT + NB) * TJ, :], x_tiles[:, TJ:, :]).then_inc(x_loaded, 16)
        prime(sp, "sync")

        def stack_parts(s):
            for hh in range(NH):
                for k, ready in enumerate((part1, part2, part3)):
                    sp.wait_ge(ready.sem, ready.at(s))
                    if k == 0:
                        hold(sp)
                        sp.wait_ge(du_spread.sem, du_spread.at(s - 1, HT * (hh + 1)))
                    hold(sp)
                    for q in range(QR):
                        sp.dma_start(stack[32 * k:32 * k + 32, q, hh, :, :],
                                     parts[32 * q:32 * q + 32, k, hh:hh + NH + 1:NH, :])\
                            .then_inc(stacked[hh].sem, 16)

        stack_parts(0)
        with sp.Fori(0, NB) as s:
            stack_parts(s + 1)
        if out is not None:
            for s in range(NB):
                sp.wait_ge(fo_added.sem, fo_added.at(s))
                sp.dma_start(out[s].rearrange("(j p) d -> p j d", p=P),
                             xr[:, TJ * (s + FRONT):TJ * (s + FRONT + 1), :]).then_inc(loaded, 16)
            sp.wait_ge(loaded, 16 * (SETUP_DMAS + NB))

    @block.tensor
    def _(pe):
        prime(pe, "tensor")
        pe.wait_ge(loaded, 16 * SETUP_DMAS)
        pe.wait_ge(setup_vec, 10)
        pe.wait_ge(setup_pool, 2)
        nc.tensor.matmul(p_y[:, :], ident, hc[:, RC - 1, :], start=True, stop=False).then_inc(setup_pe, 1)

        def turn(s):
            pe.wait_ge(a_norm.sem, a_norm.at(s))
            pe.wait_ge(uz_read.sem, uz_read.at(s - 1))
            for j in range(TJ):
                last = nc.tensor.transpose(p_a[:, j * P:(j + 1) * P], rn[:, j, :], ident)
            last.then_inc(a_turned.sem, 1)

        def project_u(s, hh, k):
            if k == 0 and hh == 0:
                pe.wait_ge(a_copied.sem, a_copied.at(s))
                pe.wait_ge(mo_read.sem, mo_read.at(s - 2))
            elif k == 0:
                pe.wait_ge(uz_read.sem, uz_read.at(s, hh))
            mm = nc.tensor.matmul(p_a[:, :], w_taps[:, k, hh * P:(hh + 1) * P], rnT[:, k:k + T],
                                  start=(k == 0), stop=(k == TAPS - 1))
            if k == TAPS - 1:
                mm.then_inc(uz_ready.sem, 1)

        def project_z(s, hh):
            if hh == 0:
                pe.wait_ge(x_read.sem, x_read.at(s))
            else:
                pe.wait_ge(uz_read.sem, uz_read.at(s, 3))
            nc.tensor.matmul(p_a[:, :], w_z[:, hh * P:(hh + 1) * P], rnT[:, TAPS - 1:],
                             start=True, stop=True).then_inc(uz_ready.sem, 1)

        def project_x(s, b, which, hh):
            if hh == 0 and which == 0:
                pe.wait_ge(uz_read.sem, uz_read.at(s, NH))
                pe.wait_ge(u_silu.sem, u_silu.at(s))
            elif hh == 0 and which == 1:
                pe.wait_ge(dtp_read.sem, dtp_read.at(s))
            elif hh == 0:
                pe.wait_ge(x_read.sem, x_read.at(s, which))
            name, n = (("xr_w", RANK), ("xb_w", P), ("xc_w", P))[which]
            mm = nc.tensor.matmul(p_a[0:n, :], W(name, NH, n)[:, hh, :], u[:, b, hh, :],
                                  start=(hh == 0), stop=(hh == NH - 1))
            if hh == NH - 1:
                mm.then_inc(x_ready.sem, 1)

        def project_dt(s, hh):
            if hh == 0:
                pe.wait_ge(x_read.sem, x_read.at(s, 1))
            else:
                pe.wait_ge(dtp_read.sem, dtp_read.at(s, hh))
            nc.tensor.matmul(p_a[:, :], W("dt_w")[0:RANK, hh * P:(hh + 1) * P], dtr[:, :],
                             start=True, stop=True).then_inc(dtp_ready.sem, 1)

        def spread_tile(s, b, i, k, bank, free, done):
            hh, j, q = i // HT, i % HT // QR, i % QR
            if i % HT == 0 and k == 0:
                pe.wait_ge(stacked[hh].sem, stacked[hh].at(s))
            pe.wait_ge(free.sem, free.at(s, i - 1))
            nc.tensor.matmul(bank[i % 2][:, :], spread_b[:, j, :], stack[:, q, hh, k, :],
                             start=True, stop=True).then_inc(done.sem, 1)

        def spread_dt(s, b, i):
            spread_tile(s, b, i, 0, p_dt, decayed, dt_spread)

        def spread_du(s, b, i):
            spread_tile(s, b, i, 1, p_du, driven, du_spread)

        def gather_y(s, k):
            hh, j = k // JT, k % JT
            if j == 0:
                pe.wait_ge(y_read.sem, y_read.at(s, hh))
            pe.wait_ge(weighed.sem, weighed.at(s, QR * (k + 1)))
            for q in range(QR):
                last = nc.tensor.matmul(p_y[32 * q:32 * q + 32, :], gather[:, j, :],
                                        hc[:, (QR * k + q) % RC, :], start=(j == 0), stop=(j == JT - 1))
            last.then_inc(gathered.sem, 1)

        def project_out(s, b, part, last_step):
            if part == 0:
                pe.wait_ge(y_done.sem, y_done.at(s))
                if last_step:
                    pe.wait_ge(uz_read.sem, uz_read.at(s + 1))
                else:
                    pe.wait_ge(a_copied.sem, a_copied.at(s + 2))
            wo = W("out_w", NH, D)
            for j in range(2 * part, 2 * part + 2):
                for hh in range(NH):
                    last = nc.tensor.matmul(p_a[:, j * D:(j + 1) * D], z[:, b, hh, j * P:(j + 1) * P],
                                            wo[:, hh, :], start=(hh == 0), stop=(hh == NH - 1))
            if part == 1:
                last.then_inc(out_done.sem, 1)

        def f_turn(s):
            pe.wait_ge(f_norm.sem, f_norm.at(s))
            pe.wait_ge(g2_read.sem, g2_read.at(s - 1))
            for j in range(TJ):
                last = nc.tensor.transpose(p_f[0][:, j * P:(j + 1) * P], fx[:, j, :], ident)
            last.then_inc(f_turned.sem, 1)

        def f_first(s, m):
            if m == 0:
                pe.wait_ge(f_copied.sem, f_copied.at(s))
                pe.wait_ge(f3_read.sem, f3_read.at(s - 1))
            elif m >= 2:
                pe.wait_ge(f1_read.sem, f1_read.at(s, m - 1))
            nc.tensor.matmul(p_f[(m + 1) % 2][:, :], W("w1")[:, m * P:(m + 1) * P], fxT[:, :],
                             start=True, stop=True).then_inc(f1_ready.sem, 1)

        def f_second(s, m):
            if m < 2:
                pe.wait_ge(f1_read.sem, f1_read.at(s, m + 3))
            else:
                pe.wait_ge(f_gated.sem, f_gated.at(s, m - 1))
            nc.tensor.matmul(p_f[(m + 1) % 2][:, :], W("w2")[:, m * P:(m + 1) * P], fxT[:, :],
                             start=True, stop=True).then_inc(f2_ready.sem, 1)

        def f_hidden1(s, m, k):
            if k == 0 and m == 0:
                pe.wait_ge(f_gated.sem, f_gated.at(s, FK - 1))
            elif k == 0 and m >= 2:
                pe.wait_ge(g1_read.sem, g1_read.at(s, m - 1))
            if (m, k) in ((0, FK - 1), (1, 0)):
                pe.wait_ge(f_gated.sem, f_gated.at(s))
            mm = nc.tensor.matmul(p_f[(m + 1) % 2][:, :], W("h1", FK, FH)[:, k, m * P:(m + 1) * P], fg[:, k, :],
                                  start=(k == 0), stop=(k == FK - 1))
            if k == FK - 1:
                mm.then_inc(g1_ready.sem, 1)

        def f_hidden2(s, m, k):
            if k == 0 and m == 0:
                pe.wait_ge(g1_gelu.sem, g1_gelu.at(s))
            elif k == 0 and m >= 2:
                pe.wait_ge(g2_read.sem, g2_read.at(s, m - 1))
            mm = nc.tensor.matmul(p_f[(m + 1) % 2][:, :], W("h2", FK, FH)[:, k, m * P:(m + 1) * P], fg[:, k, :],
                                  start=(k == 0), stop=(k == FK - 1))
            if k == FK - 1:
                mm.then_inc(g2_ready.sem, 1)

        def f_third(s, j):
            if j == 0:
                pe.wait_ge(g2_gelu.sem, g2_gelu.at(s))
            wv = W("w3", FK, D)
            for k in range(FK):
                last = nc.tensor.matmul(p_f[1][:, j * D:(j + 1) * D], fg[:, k, j * P:(j + 1) * P],
                                        wv[:, k, :], start=(k == 0), stop=(k == FK - 1))
            if j == TJ - 1:
                last.then_inc(f3_ready.sem, 1)

        def prepare(s, b, at):
            if at == 4:
                turn(s)
            if at in (12, 13, 14, 15):
                project_u(s, 0, (12, 13, 14, 15).index(at))
            if at in (17, 18, 20, 22):
                project_u(s, 1, (17, 18, 20, 22).index(at))
            if at == 26:
                project_x(s, b, 0, 0)
                project_x(s, b, 0, 1)
            if at in (28, 30):
                project_dt(s, (28, 30).index(at))
            if at in (43, 44):
                project_x(s, b, 1, (43, 44).index(at))
            if at == 46:
                project_x(s, b, 2, 0)
            if at == 47:
                project_x(s, b, 2, 1)
            if at in (62, 63):
                project_z(s, (62, 63).index(at))

        def feed(s, at):
            if at == 15:
                f_turn(s)
            if at in (16, 17, 18, 21):
                f_first(s, (16, 17, 18, 21).index(at))
            if at in (24, 25, 27, 28):
                f_second(s, (24, 25, 27, 28).index(at))
            if at in (30, 31, 32, 33, 34, 35, 36, 37, 38, 39, 40, 41, 42, 43, 44, 45):
                f_hidden1(s, *divmod((30, 31, 32, 33, 34, 35, 36, 37, 38, 39, 40, 41, 42, 43, 44, 45).index(at), FK))
            if at in (48, 49, 50, 51, 52, 53, 54, 55, 56, 57, 58, 59, 60, 61, 62, 63):
                f_hidden2(s, *divmod((48, 49, 50, 51, 52, 53, 54, 55, 56, 57, 58, 59, 60, 61, 62, 63).index(at), FK))

        def feed_end(s, at):
            if at in (4, 5, 8, 9):
                f_third(s, (4, 5, 8, 9).index(at))

        def mix_end(s, b, at, last_step=False):
            if at == 3:
                gather_y(s, NT // QR - 1)
            if at in (6, 7):
                project_out(s, b, (6, 7).index(at), last_step)

        for at in range(NT):
            prepare(0, 0, at)
        for i in range(AHEAD):
            spread_dt(0, 0, i)
        for i in range(LATER):
            spread_du(0, 0, i)
        with pe.Fori(0, NB // 2) as m:
            for b in range(2):
                s = 2 * m + b
                for i in range(NT):
                    spread_dt(*tile(s, b, i + AHEAD))
                    spread_du(*tile(s, b, i + LATER))
                    if i % QR == QR - 1 and i >= 2 * QR - 1:
                        gather_y(s, i // QR - 1)
                    mix_end(s - 1, 1 - b, i)
                    feed_end(s - 2, i)
                    prepare(s + 1, 1 - b, i)
                    feed(s - 1, i)
        for at in range(NT):
            mix_end(NB - 1, 1, at, last_step=True)
            feed_end(NB - 2, at)
            feed(NB - 1, at)
        for at in range(NT):
            feed_end(NB - 1, at)

    @block.scalar
    def _(act):
        prime(act, "scalar")
        act.wait_ge(loaded, 16 * SETUP_DMAS)
        nc.scalar.activation(a_neg[:, :], W("a_log"), ACT.Exp).then_inc(setup_act, 1)
        act.wait_ge(setup_vec, 10)
        act.wait_ge(setup_pool, 2)

        def copy_turned(s):
            act.wait_ge(a_turned.sem, a_turned.at(s))
            act.wait_ge(uz_ready.sem, uz_ready.at(s - 1))
            nc.scalar.activation(rnT[:, TAPS - 1:], p_a[:, :], ACT.Copy).then_inc(a_copied.sem, 1)

        def read_uz(s, b, k):
            act.wait_ge(uz_ready.sem, uz_ready.at(s, k + 1))
            if k in (0, NH):
                act.wait_ge(out_done.sem, out_done.at(s - 2))
            hh = k % NH
            if k < NH:
                nc.scalar.activation(u[:, b, hh, :], p_a[:, :], ACT.Identity,
                                     bias=W("conv_b")[:, hh:hh + 1]).then_inc(uz_read.sem, 1)
            else:
                nc.scalar.activation(z[:, b, hh, :], p_a[:, :], ACT.Copy).then_inc(uz_read.sem, 1)

        def silu_u(s, b):
            act.wait_ge(uz_read.sem, uz_read.at(s, NH))
            nc.scalar.activation(u[:, b, :, :], u[:, b, :, :], ACT.Silu).then_inc(u_silu.sem, 1)

        def silu_z(s, b):
            act.wait_ge(uz_read.sem, uz_read.at(s))
            nc.scalar.activation(z[:, b, :, :], z[:, b, :, :], ACT.Silu).then_inc(z_silu.sem, 1)

        def read_x(s, b, which):
            act.wait_ge(x_ready.sem, x_ready.at(s, which + 1))
            if which == 0:
                act.wait_ge(dtp_ready.sem, dtp_ready.at(s - 1))
                nc.scalar.activation(dtr[:, :], p_a[0:RANK, :], ACT.Copy).then_inc(x_read.sem, 1)
            elif which == 1:
                act.wait_ge(driven.sem, driven.at(s - 2))
                nc.scalar.activation(brep[:, b, :], p_a[:, :], ACT.Copy).then_inc(x_read.sem, 1)
            else:
                act.wait_ge(weighed.sem, weighed.at(s - 2))
                nc.scalar.activation(crep[:, b, :], p_a[:, :], ACT.Copy).then_inc(x_read.sem, 1)

        def read_dtp(s, b, hh):
            act.wait_ge(dtp_ready.sem, dtp_ready.at(s, hh + 1))
            if hh == 0:
                act.wait_ge(part3.sem, part3.at(s - 1))
                act.wait_ge(sp_rest.sem, sp_rest.at(s - 1))
            nc.scalar.activation(dd[:, 0, hh, :], p_a[:, :], ACT.Identity,
                                 bias=W("dt_b")[:, hh:hh + 1]).then_inc(dtp_read.sem, 1)

        def softplus_abs_exp(s, b):
            act.wait_ge(dtp_read.sem, dtp_read.at(s))
            act.wait_ge(stacked[1].sem, stacked[1].at(s - 1))
            nc.scalar.activation(ab[:, :, :], dd[:, 0, :, :], ACT.Abs).then_inc(sp_abs.sem, 1)
            act.wait_ge(sp_abs.sem, sp_abs.at(s))
            nc.scalar.activation(ex[:, :, :], ab[:, :, :], ACT.Exp, scale=-1.0).then_inc(sp_exp.sem, 1)

        def softplus_ln(s):
            act.wait_ge(sp_exp.sem, sp_exp.at(s))
            nc.scalar.activation(ab[:, :, :], ex[:, :, :], ACT.Ln, bias=1.0).then_inc(sp_ln.sem, 1)

        def split1(s):
            act.wait_ge(dt_done.sem, dt_done.at(s))
            nc.scalar.activation(parts[:, 0, :, :], dd[:, :, :, :], ACT.Copy).then_inc(part1.sem, 1)

        def split2(s):
            act.wait_ge(rest1.sem, rest1.at(s))
            nc.scalar.activation(parts[:, 1, :, :], dd[:, :, :, :], ACT.Copy).then_inc(part2.sem, 1)

        def decay(s, b, i):
            act.wait_ge(dt_spread.sem, dt_spread.at(s, i + 1))
            act.wait_ge(scanned.sem, scanned.at(s, i + 1 - RA))
            nc.scalar.activation(dA[:, i % RA, :], p_dt[i % 2][:, :], ACT.Exp,
                                 scale=a_neg[:, i:i + 1]).then_inc(decayed.sem, 1)

        def f_copy(s):
            act.wait_ge(f_turned.sem, f_turned.at(s))
            nc.scalar.activation(fxT[:, :], p_f[0][:, :], ACT.Copy).then_inc(f_copied.sem, 1)

        def f_read(ready, read, scale, used, used_step, s, m):
            act.wait_ge(ready.sem, ready.at(s, m + 1))
            if m == 0:
                act.wait_ge(used.sem, used.at(used_step))
            nc.scalar.activation(fr[:, m, :], p_f[(m + 1) % 2][:, :], ACT.Copy,
                                 scale=W(scale)[:, m:m + 1]).then_inc(read.sem, 1)

        def f_activate(s, read, done, to, func):
            act.wait_ge(read.sem, read.at(s))
            nc.scalar.activation(to[:, :, :], fr[:, :, :], func).then_inc(done.sem, 1)

        def prepare(s, b, at):
            if at == 4:
                copy_turned(s)
            if at in (16, 23):
                read_uz(s, b, (16, 23).index(at))
            if at == 23:
                silu_u(s, b)
            if at == 27:
                read_x(s, b, 0)
            if at in (28, 31):
                read_dtp(s, b, (28, 31).index(at))
            if at == 32:
                softplus_abs_exp(s, b)
            if at == 35:
                softplus_ln(s)
            if at == 44:
                read_x(s, b, 1)
            if at == 47:
                read_x(s, b, 2)
            if at == 49:
                split1(s)
            if at == 51:
                split2(s)
            if at in (62, 63):
                read_uz(s, b, NH + (62, 63).index(at))

        def feed(s, at):
            if at == 15:
                f_copy(s)
            if at in (17, 18, 19, 20):
                f_read(f1_ready, f1_read, "w1_s", g2_gelu, s - 1, s, (17, 18, 19, 20).index(at))
            if at == 24:
                f_activate(s, f1_read, f_silu, fr, ACT.Silu)
            if at in (34, 38, 42, 46):
                f_read(g1_ready, g1_read, "h1_s", f_gated, s, s, (34, 38, 42, 46).index(at))
            if at == 46:
                f_activate(s, g1_read, g1_gelu, fg, ACT.Gelu)
            if at in (51, 55, 59, 63):
                f_read(g2_ready, g2_read, "h2_s", g1_gelu, s, s, (51, 55, 59, 63).index(at))
            if at == 63:
                f_activate(s, g2_read, g2_gelu, fg, ACT.Gelu)

        for at in range(NT):
            prepare(0, 0, at)
        for i in range(AHEAD):
            decay(0, 0, i)
        with act.Fori(0, NB // 2) as m:
            for b in range(2):
                s = 2 * m + b
                for i in range(NT):
                    decay(*tile(s, b, i + AHEAD))
                    feed(s - 1, i)
                    prepare(s + 1, 1 - b, i)
                    if i == 23:
                        silu_z(s, b)
        for at in range(NT):
            feed(NB - 1, at)

    @block.vector
    def _(dve):
        prime(dve, "vector")
        for t in (xr[:, 0:FRONT * TJ, :], xr[:, TJ * (NB + FRONT):, :], u[:, 1, :, :], z[:, 1, :, :],
                  h[:, 1, :, :], fg[:, :, :]):
            nc.vector.memset(t, 0.0).then_inc(setup_vec, 1)
        nc.vector.memset(rnT[:, 0:TAPS - 1], 0.0).then_inc(setup_vec, 1)
        dve.wait_ge(loaded, 16 * SETUP_DMAS)
        cw = S("conv_w", TAPS, DI)
        for k in range(TAPS):
            last = nc.vector.scalar_tensor_tensor(out=w_taps[:, k, :], in0=S("in_w")[:, 0:DI],
                                                  scalar=W("norm_w"), in1=cw[:, k, :],
                                                  op0=ALU.mult, op1=ALU.mult)
        nc.vector.tensor_scalar(w_z[:, :], S("in_w")[:, DI:], W("norm_w"), None, ALU.mult)\
            .then_inc(setup_vec, 1)
        nc.vector.tensor_copy(spread_b[:, :, :], S("spread", JT, P)[0:PARTS * 32, :, :]).then_inc(setup_vec, 1)
        dve.wait_ge(setup_act, 1)
        nc.vector.tensor_scalar(a_neg[:, :], a_neg[:, :], -1.0, None, ALU.mult).then_inc(setup_vec, 1)
        dve.wait_ge(setup_vec, 10)
        dve.wait_ge(setup_pe, 1)

        def stats(s, at, src, partial, done):
            hold(dve)
            for j in range(TJ):
                last = nc.vector.bn_stats(st[:, at, j, :], src(j))
            last.then_inc(partial.sem, 1)
            dve.wait_ge(partial.sem, partial.at(s))
            hold(dve)
            for j in range(TJ):
                last = nc.vector.bn_aggr(mv[:, at, j, :], st[:, at, j, :])
            last.then_inc(done.sem, 1)

        def normalize(dst, src, at, rstd):
            for j in range(TJ):
                last = nc.vector.tensor_scalar(dst(j), src(j), mv[:, at, j, 0:1], rstd[:, j:j + 1],
                                               ALU.subtract, ALU.mult)
            return last

        def finish_half(s, b, hh):
            dve.wait_ge(gathered.sem, gathered.at(s, JT * (hh + 1)))
            dve.wait_ge(y_done.sem, y_done.at(s, hh))
            dve.wait_ge(z_silu.sem, z_silu.at(s))
            nc.vector.scalar_tensor_tensor(out=u[:, b, hh, :], in0=u[:, b, hh, :], scalar=W("d_skip")[:, hh:hh + 1],
                                           in1=p_y[:, :], op0=ALU.mult, op1=ALU.add).then_inc(y_read.sem, 1)
            dve.wait_ge(y_read.sem, y_read.at(s, hh + 1))
            nc.vector.tensor_tensor(z[:, b, hh, :], u[:, b, hh, :], z[:, b, hh, :], ALU.mult)\
                .then_inc(y_done.sem, 1)

        def mix_stats(s, b):
            dve.wait_ge(out_done.sem, out_done.at(s))
            dve.wait_ge(h_norm.sem, h_norm.at(s))
            dve.wait_ge(fo_added.sem, fo_added.at(s - 2))
            nc.vector.tensor_tensor(mo[:, :, :], h[:, b, :, :], p_a[:, :].rearrange("p (j d) -> p j d", j=TJ),
                                    ALU.add).then_inc(mo_read.sem, 1)
            dve.wait_ge(mo_read.sem, mo_read.at(s))
            stats(s, 0, lambda j: mo[:, j, :], mo_bn, mo_stats)

        def mix_add(s):
            dve.wait_ge(mo_rstd.sem, mo_rstd.at(s))
            normalize(lambda j: mo[:, j, :], lambda j: mo[:, j, :], 0, rs[:, 0, :]).then_inc(mo_norm.sem, 1)
            dve.wait_ge(mo_norm.sem, mo_norm.at(s))
            nc.vector.tensor_tensor(X(s), X(s), mo[:, :, :], ALU.add).then_inc(mo_added.sem, 1)

        def a_stat(s):
            stats(s, 1, lambda j: Xj(s, j), a_bn, a_stats)

        def a_normalize(s, b):
            dve.wait_ge(a_rstd.sem, a_rstd.at(s))
            dve.wait_ge(f_turned.sem, f_turned.at(s - 3))
            normalize(lambda j: rn[:, j, :], lambda j: Xj(s, j), 1, s2).then_inc(a_norm.sem, 1)

        def mix_in(s, b):
            dve.wait_ge(mo_read.sem, mo_read.at(s - 2))
            normalize(lambda j: h[:, b, j, :], lambda j: Xj(s, j), 1, rs[:, 1, :])\
                .then_inc(h_norm.sem, 1)

        def softplus_kept(s):
            dve.wait_ge(sp_exp.sem, sp_exp.at(s))
            dve.wait_ge(dt_done.sem, dt_done.at(s - 1))
            nc.vector.tensor_scalar(kept[:, :, :], ex[:, :, :], 1.0, 1.0, ALU.add, ALU.subtract)\
                .then_inc(sp_kept.sem, 1)
            nc.vector.tensor_scalar(dd[:, 0, :, :], dd[:, 0, :, :], 0.0, None, ALU.max).then_inc(sp_kept.sem, 1)

        def dt_finish(s, b):
            dve.wait_ge(sp_ln.sem, sp_ln.at(s))
            dve.wait_ge(sp_rest.sem, sp_rest.at(s))
            nc.vector.scalar_tensor_tensor(out=ab[:, :, :], in0=kept[:, :, :], scalar=0.0, in1=ab[:, :, :],
                                           op0=ALU.is_gt, op1=ALU.mult).then_inc(dt_done.sem, 1)

        def dt_sum(s):
            dve.wait_ge(dt_done.sem, dt_done.at(s, 1))
            nc.vector.tensor_tensor(dd[:, 0, :, :], dd[:, 0, :, :], ab[:, :, :], ALU.add)\
                .then_inc(dt_done.sem, 1)

        def dt_times_u(s, b):
            dve.wait_ge(dt_done.sem, dt_done.at(s, 2))
            dve.wait_ge(u_silu.sem, u_silu.at(s))
            nc.vector.tensor_tensor(dd[:, 1, :, :], dd[:, 0, :, :], u[:, b, :, :], ALU.mult)\
                .then_inc(dt_done.sem, 1)

        def split_rest(s):
            dve.wait_ge(part1.sem, part1.at(s))
            nc.vector.tensor_tensor(dd[:, :, :, :], dd[:, :, :, :], parts[:, 0, :, :], ALU.subtract)\
                .then_inc(rest1.sem, 1)

        def split3(s):
            dve.wait_ge(part2.sem, part2.at(s))
            nc.vector.tensor_tensor(parts[:, 2, :, :], dd[:, :, :, :], parts[:, 1, :, :], ALU.subtract)\
                .then_inc(part3.sem, 1)

        def drive(s, b, i):
            dve.wait_ge(du_spread.sem, du_spread.at(s, i + 1))
            if i == 0:
                dve.wait_ge(x_read.sem, x_read.at(s, 1))
            dve.wait_ge(scanned.sem, scanned.at(s, i + 1 - RB))
            nc.vector.tensor_tensor(dB[:, i % RB, :], p_du[i % 2][:, :], brep[:, b, :], ALU.mult)\
                .then_inc(driven.sem, 1)

        def scan(s, i):
            dve.wait_ge(decayed.sem, decayed.at(s, i + 1))
            dve.wait_ge(driven.sem, driven.at(s, i + 1))
            dve.wait_ge(weighed.sem, weighed.at(s, i + 1 - RH))
            nc.vector.tensor_tensor_scan(hs[:, i % RH, :], dA[:, i % RA, :], dB[:, i % RB, :], 0.0,
                                         ALU.mult, ALU.add).then_inc(scanned.sem, 1)

        def f_stat(s):
            dve.wait_ge(mo_added.sem, mo_added.at(s))
            stats(s, 2, lambda j: Xj(s, j), f_bn, f_stats)

        def f_normalize(s, last_step=False):
            dve.wait_ge(f_rstd.sem, f_rstd.at(s))
            if not last_step:
                dve.wait_ge(a_turned.sem, a_turned.at(s + 2))
            normalize(lambda j: fx[:, j, :], lambda j: Xj(s, j), 2, rs[:, 2, :]).then_inc(f_norm.sem, 1)

        def f_gate(s, m):
            dve.wait_ge(f2_ready.sem, f2_ready.at(s, m + 1))
            if m == 0:
                dve.wait_ge(f_silu.sem, f_silu.at(s))
                dve.wait_ge(f3_ready.sem, f3_ready.at(s - 1))
            nc.vector.scalar_tensor_tensor(out=fg[:, m, :], in0=p_f[(m + 1) % 2][:, :],
                                           scalar=W("w2_s")[:, m:m + 1], in1=fr[:, m, :],
                                           op0=ALU.mult, op1=ALU.mult).then_inc(f_gated.sem, 1)

        def f_out_stats(s, last_step):
            dve.wait_ge(f3_ready.sem, f3_ready.at(s))
            if not last_step:
                dve.wait_ge(mo_added.sem, mo_added.at(s + 1))
            nc.vector.tensor_tensor(fo[:, :, :], p_f[1][:, :].rearrange("p (j d) -> p j d", j=TJ),
                                    W("w3_s").rearrange("p (a d) -> p a d", a=1).broadcast_to([P, TJ, D]),
                                    ALU.mult).then_inc(f3_read.sem, 1)
            dve.wait_ge(f3_read.sem, f3_read.at(s))
            stats(s, 3, lambda j: fo[:, j, :], fo_bn, fo_stats)

        def f_add(s):
            dve.wait_ge(fo_rstd.sem, fo_rstd.at(s))
            normalize(lambda j: fo[:, j, :], lambda j: fo[:, j, :], 3, rs[:, 3, :]).then_inc(fo_norm.sem, 1)
            dve.wait_ge(fo_norm.sem, fo_norm.at(s))
            nc.vector.tensor_tensor(X(s), X(s), fo[:, :, :], ALU.add).then_inc(fo_added.sem, 1)

        def prepare(s, b, at):
            if at == 0:
                a_stat(s)
            if at == 2:
                a_normalize(s, b)
            if at == 12:
                mix_in(s, b)
            if at == 34:
                softplus_kept(s)
            if at == 45:
                dt_finish(s, b)
            if at == 47:
                dt_sum(s)
            if at == 47:
                dt_times_u(s, b)
            if at == 50:
                split_rest(s)
            if at == 54:
                split3(s)

        def feed(s, at, last_step=False):
            if at == 10:
                f_stat(s)
            if at == 13:
                f_normalize(s, last_step)
            if at in (24, 25, 28, 29):
                f_gate(s, (24, 25, 28, 29).index(at))

        def feed_end(s, at, last_step=False):
            if at == 12:
                f_out_stats(s, last_step)
            if at == 14:
                f_add(s)

        def mix_end(s, b, at):
            if at == 4:
                finish_half(s, b, 1)
            if at == 8:
                mix_stats(s, b)
            if at == 10:
                mix_add(s)

        for at in range(NT):
            prepare(0, 0, at)
        for i in range(LATER):
            drive(0, 0, i)
        dve.wait_ge(x_loaded, 16)
        with dve.Fori(0, NB // 2) as m:
            for b in range(2):
                s = 2 * m + b
                for i in range(NT):
                    scan(s, i)
                    drive(*tile(s, b, i + LATER))
                    if i == 38:
                        finish_half(s, b, 0)
                    feed_end(s - 2, i)
                    mix_end(s - 1, 1 - b, i)
                    prepare(s + 1, 1 - b, i)
                    feed(s - 1, i)
        for at in range(NT):
            feed_end(NB - 2, at)
            mix_end(NB - 1, 1, at)
            feed(NB - 1, at, last_step=True)
        for at in range(NT):
            feed_end(NB - 1, at, last_step=True)

    @block.gpsimd
    def _(pool):
        prime(pool, "gpsimd")
        nc.gpsimd.memset(half_neg[:, :], -0.5).then_inc(setup_pool, 1)
        nc.gpsimd.memset(hc[:, RC - QR:, :], 0.0).then_inc(setup_pool, 1)
        pool.wait_ge(setup_pool, 2)
        pool.wait_ge(setup_pe, 1)

        def rstd(s, at, stats, var, done):
            pool.wait_ge(stats.sem, stats.at(s))
            hold(pool)
            nc.gpsimd.tensor_scalar(rs[:, at, :], mv[:, at, :, 1], LN_EPS, None, ALU.add).then_inc(var.sem, 1)
            pool.wait_ge(var.sem, var.at(s, 1))
            nc.gpsimd.tensor_tensor(rs[:, at, :], rs[:, at, :], half_neg[:, :], ALU.pow).then_inc(done.sem, 1)

        def a_scales(s):
            r, v = rs[:, 1, :], mv[:, 1, :, 1]
            pool.wait_ge(a_stats.sem, a_stats.at(s))
            hold(pool)
            nc.gpsimd.tensor_scalar(r, v, LN_EPS, None, ALU.add).then_inc(a_var.sem, 1)
            pool.wait_ge(a_var.sem, a_var.at(s, 1))
            nc.gpsimd.tensor_tensor(r, r, half_neg[:, :], ALU.pow).then_inc(a_var.sem, 1)
            pool.wait_ge(a_var.sem, a_var.at(s, 2))
            nc.gpsimd.tensor_tensor(tmp[:, :], r, r, ALU.mult).then_inc(a_var.sem, 1)
            pool.wait_ge(a_var.sem, a_var.at(s, 3))
            nc.gpsimd.tensor_tensor(tmp[:, :], tmp[:, :], v, ALU.mult).then_inc(a_var.sem, 1)
            pool.wait_ge(a_var.sem, a_var.at(s, 4))
            hold(pool)
            nc.gpsimd.tensor_scalar(tmp[:, :], tmp[:, :], RMS_EPS, None, ALU.add).then_inc(a_var.sem, 1)
            pool.wait_ge(a_var.sem, a_var.at(s, 5))
            nc.gpsimd.tensor_tensor(tmp[:, :], tmp[:, :], half_neg[:, :], ALU.pow).then_inc(a_var.sem, 1)
            pool.wait_ge(a_var.sem, a_var.at(s, 6))
            nc.gpsimd.tensor_tensor(s2[:, :], tmp[:, :], r, ALU.mult).then_inc(a_rstd.sem, 1)

        def softplus_sub(s, hh):
            pool.wait_ge(sp_kept.sem, sp_kept.at(s))
            pool.wait_ge(sp_ln.sem, sp_ln.at(s))
            nc.gpsimd.tensor_tensor(ex[:, hh, :], ex[:, hh, :], kept[:, hh, :], ALU.subtract)\
                .then_inc(sp_rest.sem, 1)

        def softplus_add(s, hh):
            pool.wait_ge(sp_rest.sem, sp_rest.at(s, 1 + hh))
            nc.gpsimd.tensor_tensor(dd[:, 0, hh, :], dd[:, 0, hh, :], ex[:, hh, :], ALU.add)\
                .then_inc(sp_rest.sem, 1)

        def weigh(s, b, i):
            pool.wait_ge(scanned.sem, scanned.at(s, i + 1))
            if i == 0:
                pool.wait_ge(x_read.sem, x_read.at(s, 2))
            if i % QR == 0:
                pool.wait_ge(gathered.sem, gathered.at(s, (i - RC) // QR + 1))
            nc.gpsimd.tensor_tensor(hc[:, i % RC, :], hs[:, i % RH, :], crep[:, b, :], ALU.mult)\
                .then_inc(weighed.sem, 1)

        def prepare(s, b, at):
            if at == 0:
                a_scales(s)
            if at in (36, 38):
                softplus_sub(s, (36, 38).index(at))
            if at in (40, 42):
                softplus_add(s, (40, 42).index(at))

        def feed(s, at):
            if at == 11:
                rstd(s, 2, f_stats, f_var, f_rstd)

        def feed_end(s, at):
            if at == 12:
                rstd(s, 3, fo_stats, fo_var, fo_rstd)

        def mix_end(s, at):
            if at == 8:
                rstd(s, 0, mo_stats, mo_var, mo_rstd)

        for at in range(NT):
            prepare(0, 0, at)
        with pool.Fori(0, NB // 2) as m:
            for b in range(2):
                s = 2 * m + b
                for i in range(NT):
                    weigh(s, b, i)
                    mix_end(s - 1, i)
                    feed_end(s - 2, i)
                    prepare(s + 1, 1 - b, i)
                    feed(s - 1, i)
        for at in range(NT):
            mix_end(NB - 1, at)
            feed_end(NB - 2, at)
            feed(NB - 1, at)
        for at in range(NT):
            feed_end(NB - 1, at)


def pack(parts, width, arrays):
    out = np.zeros((P, width), np.float32)
    at = 0
    for name, n in parts:
        a = np.asarray(arrays[name], np.float32).reshape(arrays[name].shape[0], -1)
        assert a.shape[1] == n, (name, a.shape, n)
        out[:a.shape[0], at:at + n] = a
        at += n
    return out


def rows_first(a):
    return a.reshape(-1, P, a.shape[-1]).transpose(1, 0, 2)


def pack_layer0(i):
    q = np.arange(P)
    spread = np.zeros((P, JT, P), np.float32)
    gather = np.zeros((P, JT, 32), np.float32)
    for j in range(JT):
        spread[:, j, :] = (q[:, None] % 32) == DG * j + q[None, :] // NS
        gather[:, j, :] = np.arange(32)[None, :] == DG * j + q[:, None] // NS
    t = np.arange(NT)
    channel = (t // HT * P + t % QR * 32 + t % HT // QR * DG)[None, :] + (q // NS)[:, None]
    xw = i["L0_attn_x_proj_w"].T
    taps = i["L0_attn_conv_w"].T.reshape(1, -1)
    return pack(W0_PARTS, W0_WIDTH, {
        "ident": np.eye(P, dtype=np.float32),
        "norm_w": i["L0_attn_norm_w"][:, None],
        "conv_b": i["L0_attn_conv_b"].reshape(NH, P).T,
        "dt_b": i["L0_attn_dt_proj_b"].reshape(NH, P).T,
        "d_skip": i["L0_attn_D_param"].reshape(NH, P).T,
        "a_log": i["L0_attn_A_log"][channel, (q % NS)[:, None]],
        "xb_w": rows_first(np.tile(xw[:, RANK:RANK + NS], (1, DG))),
        "xc_w": rows_first(np.tile(xw[:, RANK + NS:], (1, DG))),
        "xr_w": rows_first(xw[:, :RANK]),
        "dt_w": i["L0_attn_dt_proj_w"].T,
        "out_w": rows_first(i["L0_attn_out_proj_w"].T),
        "gather": gather,
        "w1_s": i["L0_ffn_w1_s"].reshape(FK, P).T, "w2_s": i["L0_ffn_w2_s"].reshape(FK, P).T,
        "h1_s": i["L0_ffn_h1_s"].reshape(FK, P).T, "h2_s": i["L0_ffn_h2_s"].reshape(FK, P).T,
        "w3_s": np.broadcast_to(i["L0_ffn_w3_s"][None, :], (P, D)),
        "w1": i["L0_ffn_w1_w"].T, "w2": i["L0_ffn_w2_w"].T,
        "h1": rows_first(i["L0_ffn_h1_w"].T), "h2": rows_first(i["L0_ffn_h2_w"].T),
        "w3": rows_first(i["L0_ffn_w3_w"].T),
    }), pack(S0_PARTS, S0_WIDTH, {
        "in_w": i["L0_attn_in_proj_w"].T,
        "conv_w": np.broadcast_to(taps, (P, taps.shape[1])),
        "spread": spread,
    })


SH = 16
VH = SH // 2
HD = D // SH
VD = D // VH
HG = 4
GH = SH // HG
KR = PARTS * PARTS * HD
KM = KR + PARTS
BLOCKS = HG * TJ
AT = BLOCKS * GH
LAM_INIT = float(0.8 - 0.6 * np.exp(-0.3 * 12))

W1_PARTS = [("ident", P), ("wq", D), ("wk", D), ("wv", D), ("wo", D), ("ln_g", 1), ("ln_b", 1),
            ("lam", 4 * HD)]
W1_COLS, W1_WIDTH = columns(W1_PARTS)


def layer1_attention(nc, ctx, sems, passed, w2, w2_loaded, w2_in, w1_in, scratch, xr, out, NB):

    def sb(name, shape, dtype=F32):
        return ctx.enter_context(nc.sbuf_tensor(name, shape, dtype))

    def pb(name, shape):
        return ctx.enter_context(nc.psum_tensor(name, shape, F32))

    def sem(name):
        return sems.enter_context(nc.semaphore(name))

    signals = {e: [] for e in ("vector", "scalar", "tensor", "gpsimd", "sync")}

    def signal(engine, name, per=1, early=0, lead=LEAD):
        s = Signal(sem(name), per, lead)
        s.start = lead * per - early
        signals[engine].append(s)
        return s

    def prime(eng, engine):
        for s in signals[engine]:
            eng.sem_inc(s.sem, s.start)

    w = sb("w1", [P, W1_WIDTH])

    def W(name):
        a, n = W1_COLS[name]
        return w[:, a:a + n]

    ident = W("ident")

    st = sb("l1_stats", [P, 2, TJ, 6])
    mv = sb("l1_mean_var", [P, 2, TJ, 2])
    rs = sb("l1_rstd", [P, 2, TJ])
    minus_half = sb("l1_minus_half", [P, TJ * VH])
    xn = sb("att_in", [P, TJ, D])
    xT = sb("att_in_T", [P, 2, T])
    qk = sb("q_k", [P, 2, T])
    qkp = sb("q_k_parts", [P, 2, PARTS, T], BF16)
    qs = sb("q_stack", [KM, 2, SH, T], BF16)
    ks = sb("k_stack", [KM, 2, SH, T], BF16)
    va = sb("v_and_one", [P, 2, TJ, VH, 32])
    RP = 8
    pt = sb("probs_T", [P, RP, T])
    mx = sb("row_max", [P, TJ, SH])
    nm = sb("minus_max", [SH, T])
    nmp = sb("minus_max_parts", [SH, PARTS, T], BF16)
    ot = sb("out_T", [P, T])
    rc = sb("out_recip", [P, TJ, GH])
    t0 = sb("out_0", [P, TJ, 2, VD])
    t1 = sb("out_1", [P, TJ, 2, VD])
    og = sb("out_heads", [P, TJ * VH, VD])
    sq = sb("out_square", [P, TJ * VH, VD])
    hm = sb("head_sum", [P, TJ * VH])
    hv = sb("head_rstd", [P, TJ * VH])
    ogT = sb("out_normed_T", [P, T])
    ao = sb("att_out", [P, TJ, D])
    ones = sb("ones", [PARTS, T], BF16)
    lam = sb("lam_terms", [P, 2, HD])
    lsum = sb("lam_sums", [P, 2])
    nlam = sb("minus_lam", [P, 1])

    p_st = [pb(f"p_scores_T{k}", [P, T]) for k in range(2)]
    p_s = [pb(f"p_scores{k}", [P, T]) for k in range(3)]
    p_o = pb("p_out", [P, T])
    p_t = pb("p_out_turned", [P, T])
    p_m = pb("p_misc", [P, T])

    loaded = sem("l1_loaded")
    ones_set = sem("ones_set")
    set_vec = sem("l1_set_vec")
    set_act = sem("l1_set_act")
    set_pe = sem("l1_set_pe")
    SET_VEC = 9
    def hold(eng):
        eng.sem_inc(passed, 1)

    x_stats = signal("vector", "x_stats", 2)
    x_rstd = signal("gpsimd", "x_rstd", 2)
    x_norm = signal("vector", "x_norm")
    x_turned = signal("tensor", "x_turned")
    x_copied = signal("scalar", "x_copied")
    qk_ready = signal("tensor", "qk_ready", 2)
    qk_read = signal("scalar", "qk_read", 2)
    qk_part1 = signal("scalar", "qk_part1")
    qk_rest1 = signal("gpsimd", "qk_rest1")
    qk_part2 = signal("scalar", "qk_part2")
    qk_part3 = signal("gpsimd", "qk_part3")
    qk_saved = signal("sync", "qk_saved", 32)
    stacked = [signal("sync", f"qk_stacked{g}", 16 * 2 * PARTS) for g in range(HG)]
    v_ready = signal("tensor", "v_ready")
    v_read = signal("scalar", "v_read")
    s_ready = signal("tensor", "s_ready", AT, lead=LEAD + 2)
    maxed = signal("vector", "maxed", AT, lead=LEAD + 2)
    m_turned = signal("tensor", "m_turned")
    m_done = signal("vector", "m_done", 5)
    m_stacked = signal("sync", "m_stacked", 16 * PARTS)
    st_ready = signal("tensor", "st_ready", AT)
    exped = signal("scalar", "exped", AT)
    pv_done = signal("tensor", "pv_done", BLOCKS)
    o_read = signal("scalar", "o_read", HG, 1)
    o_turned = signal("tensor", "o_turned", HG, 1)
    o_comb = signal("vector", "o_comb", 4 * HG, 4)
    h_sum = signal("vector", "h_sum", 1, 1)
    h_cent = signal("vector", "h_cent", 1, 1)
    h_sq = signal("gpsimd", "h_sq", 1, 1)
    h_var = signal("vector", "h_var", 1, 1)
    h_eps = signal("gpsimd", "h_eps", 1, 1)
    h_rstd = signal("gpsimd", "h_rstd", 1, 1)
    h_norm = signal("gpsimd", "h_normed", 1, 1)
    h_turned = signal("tensor", "h_turned", 1, 1)
    h_read = signal("vector", "h_read", 1, 1)
    ao_ready = signal("tensor", "ao_ready", 1, 1)
    ao_read = signal("scalar", "ao_read", 1, 1)
    ao_stats = signal("vector", "ao_stats", 2, 2)
    ao_rstd = signal("gpsimd", "ao_rstd", 2, 2)
    ao_norm = signal("vector", "ao_norm", 1, 1)
    ao_added = signal("gpsimd", "ao_added", 1, 1)

    def X(s):
        return xr[:, bass.ds((s + FRONT) * TJ, TJ), :]

    def Xj(s, j):
        return xr[:, bass.ds((s + FRONT) * TJ + j, 1), :].rearrange("p a d -> p (a d)")

    def score_tiles(n):
        return range(5 * n, min(5 * (n + 1), AT))

    def place(i):
        return i // (TJ * GH), i // GH % TJ, i // (TJ * GH) * GH + i % GH

    block = ctx.enter_context(nc.Block())

    @block.sync
    def _(sp):
        sp.dma_start(w[:, :], w1_in).then_inc(loaded, 16)
        sp.dma_start(w2[:, :], w2_in).then_inc(w2_loaded, 16)
        prime(sp, "sync")

        def save(s, b):
            sp.wait_ge(qk_part3.sem, qk_part3.at(s))
            hold(sp)
            sp.wait_ge(qk_part2.sem, qk_part2.at(s))
            hold(sp)
            sp.wait_ge(stacked[HG - 1].sem, stacked[HG - 1].at(s - 2))
            hold(sp)
            for c in range(2):
                sp.dma_start(scratch[b, c].rearrange("k f t -> f k t"), qkp[:, c, :, :])\
                    .then_inc(qk_saved.sem, 16)

        def load(s, b, g):
            if g == 0:
                sp.wait_ge(qk_saved.sem, qk_saved.at(s))
                hold(sp)
            sp.wait_ge(pv_done.sem, pv_done.at(s - 2, TJ * (g + 1)))
            hold(sp)
            sp.wait_ge(s_ready.sem, s_ready.at(s - 1, TJ * GH * g + 1))
            hold(sp)
            heads = slice(g * GH, (g + 1) * GH)
            q_in = scratch[b, 0].rearrange("k (d h) t -> k d h t", h=SH)
            k_in = scratch[b, 1].rearrange("k (d h) t -> (k d) h t", h=SH)
            n = PARTS * HD
            for k in range(PARTS):
                sp.dma_start(ks[n * k:n * (k + 1), b, heads, :], k_in[:, heads, :])\
                    .then_inc(stacked[g].sem, 16)
                sp.dma_start(qs[n * k:n * (k + 1), b, heads, :],
                             q_in[k:k + 1, :, heads, :].broadcast_to([PARTS, HD, GH, T]))\
                    .then_inc(stacked[g].sem, 16)

        def stack_max(s, b):
            sp.wait_ge(pv_done.sem, pv_done.at(s - 2))
            for k in range(PARTS):
                hold(sp)
                sp.wait_ge(m_done.sem, m_done.at(s, (2, 4, 5)[k]))
                hold(sp)
                sp.dma_start(qs[KR + k:KR + k + 1, b, :, :], nmp[:, k, :]).then_inc(m_stacked.sem, 16)

        sp.wait_ge(set_vec, SET_VEC)
        hold(sp)
        for b in range(2):
            sp.dma_start(ks[KR:KM, b, :, :], ones[:, :].unsqueeze(1).broadcast_to([PARTS, SH, T]))\
                .then_inc(ones_set, 16)
        save(0, 0)
        for g in range(HG):
            load(0, 0, g)
        save(1, 1)
        for g in range(HG):
            load(1, 1, g)
        stack_max(0, 0)
        with sp.Fori(0, NB // 2) as m:
            for b in range(2):
                s = 2 * m + b
                save(s + 2, b)
                for g in range(HG - 1):
                    load(s + 2, b, g)
                stack_max(s + 1, 1 - b)
                load(s + 2, b, HG - 1)
        if out is not None:
            for s in range(NB):
                sp.wait_ge(ao_added.sem, ao_added.at(s))
                sp.dma_start(out[s].rearrange("(j p) d -> p j d", p=P),
                             xr[:, TJ * (s + FRONT):TJ * (s + FRONT + 1), :]).then_inc(loaded, 16)
            sp.wait_ge(loaded, 16 * (1 + NB))
        sp.wait_ge(qk_saved.sem, qk_saved.at(NB + 1))
        for g in range(HG):
            sp.wait_ge(stacked[g].sem, stacked[g].at(NB + 1))
        sp.wait_ge(m_stacked.sem, m_stacked.at(NB))

    @block.tensor
    def _(pe):
        prime(pe, "tensor")
        pe.wait_ge(loaded, 16)
        pe.wait_ge(set_vec, SET_VEC)
        nc.tensor.matmul(p_o[:, :], ident, pt[:, 0, :], start=True, stop=True).then_inc(set_pe, 1)

        def x_turn(s):
            pe.wait_ge(x_norm.sem, x_norm.at(s))
            pe.wait_ge(qk_read.sem, qk_read.at(s - 1))
            pe.wait_ge(v_read.sem, v_read.at(s - 2))
            for j in range(TJ):
                last = nc.tensor.transpose(p_m[:, j * P:(j + 1) * P], xn[:, j, :], ident)
            last.then_inc(x_turned.sem, 1)

        def project_qk(s, b, c):
            if c == 0:
                pe.wait_ge(x_copied.sem, x_copied.at(s))
            else:
                pe.wait_ge(qk_read.sem, qk_read.at(s, 1))
            nc.tensor.matmul(p_m[:, :], W("wk" if c else "wq"), xT[:, b, :], start=True, stop=True)\
                .then_inc(qk_ready.sem, 1)

        def project_v(s, b):
            pe.wait_ge(m_done.sem, m_done.at(s, 1))
            for j in range(TJ):
                last = nc.tensor.matmul(p_m[:, j * P:(j + 1) * P], xT[:, b, j * P:(j + 1) * P], W("wv"),
                                        start=True, stop=True)
            last.then_inc(v_ready.sem, 1)

        def score(s, b, i):
            g, j, h = place(i)
            if i % (TJ * GH) == 0:
                pe.wait_ge(stacked[g].sem, stacked[g].at(s))
            pe.wait_ge(maxed.sem, maxed.at(s, i - 2) if i >= 3 else maxed.at(s - 1))
            nc.tensor.matmul(p_s[i % 3][:, :], qs[0:KR, b, h, j * P:(j + 1) * P], ks[0:KR, b, h, :],
                             start=True, stop=True).then_inc(s_ready.sem, 1)

        def turn_max(s):
            pe.wait_ge(maxed.sem, maxed.at(s))
            pe.wait_ge(qk_read.sem, qk_read.at(s + 1))
            pe.wait_ge(ao_read.sem, ao_read.at(s - 2))
            for j in range(TJ):
                last = nc.tensor.transpose(p_m[0:SH, j * P:(j + 1) * P], mx[:, j, :], ident)
            last.then_inc(m_turned.sem, 1)

        def score_T(s, b, i):
            g, j, h = place(i)
            if i == 0:
                pe.wait_ge(m_stacked.sem, m_stacked.at(s))
            pe.wait_ge(exped.sem, exped.at(s, i - 1))
            nc.tensor.matmul(p_st[i % 2][:, :], ks[:, b, h, j * P:(j + 1) * P], qs[:, b, h, :],
                             start=True, stop=True).then_inc(st_ready.sem, 1)

        def weigh_values(s, b, n):
            g, j = n // TJ, n % TJ
            pe.wait_ge(exped.sem, exped.at(s, GH * (n + 1)))
            if n == 0:
                pe.wait_ge(v_read.sem, v_read.at(s))
            if j == 0:
                pe.wait_ge(o_read.sem, o_read.at(s, g))
            for a in range(GH):
                last = nc.tensor.matmul(p_o[32 * a:32 * a + 32, :], va[:, b, j, g * GH // 2 + a // 2, :],
                                        pt[:, (GH * n + a) % RP, :], start=(j == 0), stop=(j == TJ - 1))
            last.then_inc(pv_done.sem, 1)

        def turn_out(s, g):
            pe.wait_ge(o_read.sem, o_read.at(s, g + 1))
            pe.wait_ge(o_comb.sem, o_comb.at(s, 4 * g))
            for j in range(TJ):
                last = nc.tensor.transpose(p_t[:, j * P:(j + 1) * P], ot[:, j * P:(j + 1) * P], ident)
            last.then_inc(o_turned.sem, 1)

        def turn_heads(s, last_step):
            pe.wait_ge(h_norm.sem, h_norm.at(s))
            if not last_step:
                pe.wait_ge(qk_read.sem, qk_read.at(s + 3))
            ogf = og[:, :, :].rearrange("p (j h) d -> p j (h d)", j=TJ)
            for j in range(TJ):
                last = nc.tensor.transpose(p_m[:, j * P:(j + 1) * P], ogf[:, j, :], ident)
            last.then_inc(h_turned.sem, 1)

        def project_out(s):
            pe.wait_ge(h_read.sem, h_read.at(s))
            for j in range(TJ):
                last = nc.tensor.matmul(p_m[:, j * P:(j + 1) * P], ogT[:, j * P:(j + 1) * P], W("wo"),
                                        start=True, stop=True)
            last.then_inc(ao_ready.sem, 1)

        def prepare2(s, b, n):
            if n == 3:
                x_turn(s)
            if n in (4, 5):
                project_qk(s, b, (4, 5).index(n))

        def prepare1(s, b, n):
            if n == 13:
                turn_max(s)
            if n == 15:
                project_v(s, b)

        def finish(s, n, last_step=False):
            if n == 2:
                turn_out(s, HG - 1)
            if n == 8:
                turn_heads(s, last_step)
            if n == 9:
                project_out(s)

        for n in range(BLOCKS):
            prepare2(0, 0, n)
        for n in range(BLOCKS):
            prepare2(1, 1, n)
            for i in score_tiles(n):
                score(0, 0, i)
            prepare1(0, 0, n)
        pe.wait_ge(ones_set, 32)
        with pe.Fori(0, NB // 2) as m:
            for b in range(2):
                s = 2 * m + b
                for n in range(BLOCKS):
                    plain = list(score_tiles(n))
                    for a in range(GH):
                        score_T(s, b, GH * n + a)
                        for i in plain[a:a + 1]:
                            score(s + 1, 1 - b, i)
                        if n >= 1 and a == 1:
                            weigh_values(s, b, n - 1)
                    prepare2(s + 2, b, n)
                    finish(s - 1, n)
                    if n in (6, 10, 13):
                        turn_out(s, (6, 10, 13).index(n))
                    for i in plain[GH:]:
                        score(s + 1, 1 - b, i)
                    prepare1(s + 1, 1 - b, n)
                weigh_values(s, b, BLOCKS - 1)
        for n in range(BLOCKS):
            finish(NB - 1, n, last_step=True)

    @block.scalar
    def _(act):
        prime(act, "scalar")
        act.wait_ge(set_vec, 2)
        nc.scalar.activation(lsum[:, :], lsum[:, :], ACT.Exp).then_inc(set_act, 1)
        act.wait_ge(set_vec, SET_VEC)
        act.wait_ge(set_pe, 1)

        def x_copy(s, b):
            act.wait_ge(x_turned.sem, x_turned.at(s))
            act.wait_ge(v_ready.sem, v_ready.at(s - 2))
            nc.scalar.activation(xT[:, b, :], p_m[:, :], ACT.Copy).then_inc(x_copied.sem, 1)

        def qk_copy(s, c):
            act.wait_ge(qk_ready.sem, qk_ready.at(s, c + 1))
            act.wait_ge(qk_part3.sem, qk_part3.at(s - 1))
            nc.scalar.activation(qk[:, c, :], p_m[:, :], ACT.Copy, scale=1.0 if c else float(HD ** -0.5))\
                .then_inc(qk_read.sem, 1)

        def part1(s):
            act.wait_ge(qk_read.sem, qk_read.at(s))
            act.wait_ge(qk_saved.sem, qk_saved.at(s - 1))
            nc.scalar.activation(qkp[:, :, 0, :], qk[:, :, :], ACT.Copy).then_inc(qk_part1.sem, 1)

        def part2(s):
            act.wait_ge(qk_rest1.sem, qk_rest1.at(s))
            nc.scalar.activation(qkp[:, :, 1, :], qk[:, :, :], ACT.Copy).then_inc(qk_part2.sem, 1)

        def v_copy(s, b):
            act.wait_ge(v_ready.sem, v_ready.at(s))
            act.wait_ge(pv_done.sem, pv_done.at(s - 2))
            nc.scalar.activation(va[:, b, :, :, 0:VD].rearrange("p j h d -> p (j h) d"),
                                 p_m[:, :].rearrange("p (a d) -> p a d", d=VD), ACT.Copy)\
                .then_inc(v_read.sem, 1)

        def exps(s, i):
            act.wait_ge(st_ready.sem, st_ready.at(s, i + 1))
            if i % GH == 0:
                act.wait_ge(pv_done.sem, pv_done.at(s, i // GH - 1))
            nc.scalar.activation(pt[:, i % RP, :], p_st[i % 2][:, :], ACT.Exp).then_inc(exped.sem, 1)

        def o_copy(s, g):
            act.wait_ge(pv_done.sem, pv_done.at(s, TJ * (g + 1)))
            act.wait_ge(o_turned.sem, o_turned.at(s, g))
            nc.scalar.activation(ot[:, :], p_o[:, :], ACT.Copy).then_inc(o_read.sem, 1)

        def ao_copy(s):
            act.wait_ge(ao_ready.sem, ao_ready.at(s))
            act.wait_ge(ao_added.sem, ao_added.at(s - 1))
            nc.scalar.activation(ao[:, :, :], p_m[:, :].rearrange("p (j d) -> p j d", j=TJ), ACT.Copy)\
                .then_inc(ao_read.sem, 1)

        def prepare2(s, b, n):
            if n == 3:
                x_copy(s, b)
            if n in (4, 5):
                qk_copy(s, (4, 5).index(n))
            if n == 6:
                part1(s)
            if n == 8:
                part2(s)

        def prepare1(s, b, n):
            if n == 15:
                v_copy(s, b)

        def finish(s, n):
            if n == 0:
                o_copy(s, HG - 1)
            if n == 9:
                ao_copy(s)

        for n in range(BLOCKS):
            prepare2(0, 0, n)
        for n in range(BLOCKS):
            prepare2(1, 1, n)
            prepare1(0, 0, n)
        with act.Fori(0, NB // 2) as m:
            for b in range(2):
                s = 2 * m + b
                for n in range(BLOCKS):
                    if n in (5, 9, 13):
                        o_copy(s, (5, 9, 13).index(n))
                    for a in range(GH):
                        exps(s, GH * n + a)
                    prepare2(s + 2, b, n)
                    finish(s - 1, n)
                    prepare1(s + 1, 1 - b, n)
        for n in range(BLOCKS):
            finish(NB - 1, n)

    @block.vector
    def _(dve):
        prime(dve, "vector")
        dve.wait_ge(loaded, 16)
        terms = W("lam").rearrange("p (a k d) -> p a k d", a=2, k=2)
        nc.vector.tensor_tensor(lam[:, :, :], terms[:, 0, :, :], terms[:, 1, :, :], ALU.mult).then_inc(set_vec, 1)
        dve.wait_ge(set_vec, 1)
        nc.vector.tensor_reduce(lsum[:, :], lam[:, :, :], AX.X, ALU.add).then_inc(set_vec, 1)
        dve.wait_ge(set_act, 1)
        nc.vector.scalar_tensor_tensor(out=nlam[:, :], in0=lsum[:, 1:2], scalar=-LAM_INIT, in1=lsum[:, 0:1],
                                       op0=ALU.add, op1=ALU.subtract).then_inc(set_vec, 1)
        nc.vector.memset(va[:, :, :, :, :], 0.0).then_inc(set_vec, 1)
        dve.wait_ge(set_vec, 4)
        nc.vector.memset(va[:, :, :, :, VD:VD + 1], 1.0).then_inc(set_vec, 1)
        nc.vector.memset(pt[:, 0, :], 1.0).then_inc(set_vec, 1)
        nc.vector.memset(og[:, :, :], 0.0).then_inc(set_vec, 1)
        nc.vector.memset(ones[:, :], 1.0).then_inc(set_vec, 1)
        nc.vector.memset(minus_half[:, :], -0.5).then_inc(set_vec, 1)
        dve.wait_ge(set_vec, SET_VEC)
        dve.wait_ge(set_pe, 1)

        def stats(s, at, src, done):
            hold(dve)
            for j in range(TJ):
                last = nc.vector.bn_stats(st[:, at, j, :], src(j))
            last.then_inc(done.sem, 1)
            dve.wait_ge(done.sem, done.at(s, 1))
            hold(dve)
            for j in range(TJ):
                last = nc.vector.bn_aggr(mv[:, at, j, :], st[:, at, j, :])
            last.then_inc(done.sem, 1)

        def normalize(dst, src, at):
            for j in range(TJ):
                last = nc.vector.tensor_scalar(dst(j), src(j), mv[:, at, j, 0:1], rs[:, at, j:j + 1],
                                               ALU.subtract, ALU.mult)
            return last

        def x_stat(s):
            dve.wait_ge(x_norm.sem, x_norm.at(s - 1))
            stats(s, 0, lambda j: Xj(s, j), x_stats)

        def x_normalize(s):
            dve.wait_ge(x_rstd.sem, x_rstd.at(s))
            dve.wait_ge(x_turned.sem, x_turned.at(s - 1))
            normalize(lambda j: xn[:, j, :], lambda j: Xj(s, j), 0).then_inc(x_norm.sem, 1)

        def row_max(s, i):
            g, j, h = place(i)
            dve.wait_ge(s_ready.sem, s_ready.at(s, i + 1))
            if i == 0:
                dve.wait_ge(m_turned.sem, m_turned.at(s - 1))
            nc.vector.tensor_reduce(mx[:, j, h:h + 1], p_s[i % 3][:, :], AX.X, ALU.max).then_inc(maxed.sem, 1)

        def split_max(s):
            dve.wait_ge(m_turned.sem, m_turned.at(s))
            dve.wait_ge(m_stacked.sem, m_stacked.at(s - 1))
            nc.vector.tensor_scalar(nm[:, :], p_m[0:SH, :], -1.0, None, ALU.mult).then_inc(m_done.sem, 1)
            dve.wait_ge(m_done.sem, m_done.at(s, 1))
            nc.vector.tensor_copy(nmp[:, 0, :], nm[:, :]).then_inc(m_done.sem, 1)
            dve.wait_ge(m_done.sem, m_done.at(s, 2))
            nc.vector.tensor_tensor(nm[:, :], nm[:, :], nmp[:, 0, :], ALU.subtract).then_inc(m_done.sem, 1)
            dve.wait_ge(m_done.sem, m_done.at(s, 3))
            nc.vector.tensor_copy(nmp[:, 1, :], nm[:, :]).then_inc(m_done.sem, 1)
            dve.wait_ge(m_done.sem, m_done.at(s, 4))
            nc.vector.tensor_tensor(nmp[:, 2, :], nm[:, :], nmp[:, 1, :], ALU.subtract).then_inc(m_done.sem, 1)

        pv = p_t[:, :].rearrange("p (j a c) -> p j a c", j=TJ, a=GH)

        def combine_recip(s, g):
            dve.wait_ge(o_turned.sem, o_turned.at(s, g + 1))
            dve.wait_ge(o_comb.sem, o_comb.at(s, 4 * g))
            hold(dve)
            nc.vector.reciprocal(rc[:, :, :], pv[:, :, :, VD]).then_inc(o_comb.sem, 1)

        def combine_scale(s, g):
            dve.wait_ge(o_comb.sem, o_comb.at(s, 4 * g + 1))
            hold(dve)
            nc.vector.tensor_tensor(t0[:, :, :, :], pv[:, :, 0::2, 0:VD],
                                    rc[:, :, 0::2].unsqueeze(3).broadcast_to([P, TJ, 2, VD]), ALU.mult)\
                .then_inc(o_comb.sem, 1)
            nc.vector.scalar_tensor_tensor(out=t1[:, :, :, :], in0=pv[:, :, 1::2, 0:VD], scalar=nlam[:, :],
                                           in1=rc[:, :, 1::2].unsqueeze(3).broadcast_to([P, TJ, 2, VD]),
                                           op0=ALU.mult, op1=ALU.mult).then_inc(o_comb.sem, 1)

        def combine_sum(s, g):
            dve.wait_ge(o_comb.sem, o_comb.at(s, 4 * g + 3))
            if g == 0:
                dve.wait_ge(h_turned.sem, h_turned.at(s - 1))
            nc.vector.tensor_tensor(og[:, :, :].rearrange("p (j h) d -> p j h d", j=TJ)[:, :, 2 * g:2 * g + 2, :],
                                    t0[:, :, :, :], t1[:, :, :, :], ALU.add).then_inc(o_comb.sem, 1)

        def sum_heads(s):
            dve.wait_ge(o_comb.sem, o_comb.at(s))
            dve.wait_ge(h_cent.sem, h_cent.at(s - 1))
            nc.vector.tensor_reduce(hm[:, :], og[:, :, :], AX.X, ALU.add).then_inc(h_sum.sem, 1)

        def center_heads(s):
            dve.wait_ge(h_sum.sem, h_sum.at(s))
            nc.vector.scalar_tensor_tensor(out=og[:, :, :], in0=hm[:, :].unsqueeze(2).broadcast_to([P, TJ * VH, VD]),
                                           scalar=-1.0 / VD, in1=og[:, :, :], op0=ALU.mult, op1=ALU.add)\
                .then_inc(h_cent.sem, 1)

        def head_var(s):
            dve.wait_ge(h_sq.sem, h_sq.at(s))
            dve.wait_ge(h_norm.sem, h_norm.at(s - 1))
            nc.vector.tensor_reduce(hv[:, :], sq[:, :, :], AX.X, ALU.add).then_inc(h_var.sem, 1)

        def read_heads(s):
            dve.wait_ge(h_turned.sem, h_turned.at(s))
            dve.wait_ge(ao_ready.sem, ao_ready.at(s - 1))
            nc.vector.tensor_scalar(ogT[:, :], p_m[:, :], W("ln_g"), W("ln_b"), ALU.mult, ALU.add)\
                .then_inc(h_read.sem, 1)

        def out_stats(s):
            dve.wait_ge(ao_read.sem, ao_read.at(s))
            dve.wait_ge(ao_norm.sem, ao_norm.at(s - 1))
            stats(s, 1, lambda j: ao[:, j, :], ao_stats)

        def out_normalize(s):
            dve.wait_ge(ao_rstd.sem, ao_rstd.at(s))
            normalize(lambda j: ao[:, j, :], lambda j: ao[:, j, :], 1).then_inc(ao_norm.sem, 1)

        def side(s, n, k):
            if (n, k) == (0, 3):
                x_stat(s + 2)
            if (n, k) == (2, 0):
                x_normalize(s + 2)
            finish(s - 1, n, k)
            if n in (9, 12, 15) and k < 3:
                combine(s, (9, 12, 15).index(n), k)

        def combine(s, g, k):
            (combine_recip, combine_scale, combine_sum)[k](s, g)

        def finish(s, n, k):
            if n == 3 and k < 3:
                combine(s, HG - 1, k)
            if (n, k) == (3, 2):
                sum_heads(s)
            if (n, k) == (4, 1):
                center_heads(s)
            if (n, k) == (4, 4):
                head_var(s)
            if (n, k) == (9, 0):
                read_heads(s)
            if (n, k) == (12, 2):
                out_stats(s)
            if (n, k) == (13, 1):
                out_normalize(s)

        def maxima(s, n, k):
            if k < len(score_tiles(n)):
                row_max(s, score_tiles(n)[k])
            if (n, k) == (14, 2):
                split_max(s)

        for s in range(2):
            x_stat(s)
            x_normalize(s)
        for n in range(BLOCKS):
            for k in range(5):
                maxima(0, n, k)
        with dve.Fori(0, NB // 2) as m:
            for b in range(2):
                s = 2 * m + b
                for n in range(BLOCKS):
                    for k in range(5):
                        maxima(s + 1, n, k)
                        side(s, n, k)
        for n in range(BLOCKS):
            for k in range(5):
                finish(NB - 1, n, k)

    @block.gpsimd
    def _(pool):
        prime(pool, "gpsimd")
        pool.wait_ge(set_vec, SET_VEC)

        def rstd(s, at, stats, done):
            pool.wait_ge(stats.sem, stats.at(s))
            hold(pool)
            nc.gpsimd.tensor_scalar(rs[:, at, :], mv[:, at, :, 1], LN_EPS, None, ALU.add).then_inc(done.sem, 1)
            pool.wait_ge(done.sem, done.at(s, 1))
            nc.gpsimd.tensor_tensor(rs[:, at, :], rs[:, at, :], minus_half[:, 0:TJ], ALU.pow).then_inc(done.sem, 1)

        def square_heads(s):
            pool.wait_ge(h_cent.sem, h_cent.at(s))
            nc.gpsimd.tensor_tensor(sq[:, :, :], og[:, :, :], og[:, :, :], ALU.mult).then_inc(h_sq.sem, 1)

        def scale_heads(s):
            pool.wait_ge(h_var.sem, h_var.at(s))
            hold(pool)
            nc.gpsimd.tensor_scalar(hv[:, :], hv[:, :], 1.0 / VD, LN_EPS, ALU.mult, ALU.add).then_inc(h_eps.sem, 1)
            pool.wait_ge(h_eps.sem, h_eps.at(s))
            nc.gpsimd.tensor_tensor(hv[:, :], hv[:, :], minus_half[:, :], ALU.pow).then_inc(h_rstd.sem, 1)
            pool.wait_ge(h_rstd.sem, h_rstd.at(s))
            nc.gpsimd.tensor_tensor(og[:, :, :], og[:, :, :], hv[:, :].unsqueeze(2).broadcast_to([P, TJ * VH, VD]),
                                    ALU.mult).then_inc(h_norm.sem, 1)

        def rest1(s):
            pool.wait_ge(qk_part1.sem, qk_part1.at(s))
            nc.gpsimd.tensor_tensor(qk[:, :, :], qk[:, :, :], qkp[:, :, 0, :], ALU.subtract)\
                .then_inc(qk_rest1.sem, 1)

        def part3(s):
            pool.wait_ge(qk_part2.sem, qk_part2.at(s))
            nc.gpsimd.tensor_tensor(qkp[:, :, 2, :], qk[:, :, :], qkp[:, :, 1, :], ALU.subtract)\
                .then_inc(qk_part3.sem, 1)

        def add(s):
            pool.wait_ge(ao_norm.sem, ao_norm.at(s))
            hold(pool)
            nc.gpsimd.tensor_tensor(X(s), X(s), ao[:, :, :], ALU.add).then_inc(ao_added.sem, 1)

        def split(s):
            rest1(s)
            part3(s)

        def heads(s):
            square_heads(s)
            scale_heads(s)

        def finish(s):
            rstd(s, 1, ao_stats, ao_rstd)
            add(s)

        for s in range(2):
            rstd(s, 0, x_stats, x_rstd)
            split(s)
        with pool.Fori(0, NB) as s:
            rstd(s + 2, 0, x_stats, x_rstd)
            heads(s - 1)
            split(s + 2)
            finish(s - 1)
        heads(NB - 1)
        finish(NB - 1)


def pack_layer1(i):
    by_dim = lambda a: a.reshape(D, SH, HD).transpose(0, 2, 1).reshape(D, D)
    lam = np.stack([i[f"L1_attn_{n}"] for n in ("lq1", "lq2", "lk1", "lk2")]).reshape(1, -1)
    return pack(W1_PARTS, W1_WIDTH, {
        "ident": np.eye(P, dtype=np.float32),
        "wq": by_dim(i["L1_attn_Wq"]), "wk": by_dim(i["L1_attn_Wk"]), "wv": i["L1_attn_Wv"],
        "wo": i["L1_attn_Wo"], "ln_g": i["L1_attn_ln_g"][np.arange(P) % VD][:, None],
        "ln_b": i["L1_attn_ln_b"][np.arange(P) % VD][:, None],
        "lam": np.broadcast_to(lam, (P, lam.shape[1])),
    })


EX = 32
EH = 64
PAIR = P // EH
ET = EX // PAIR
MT = ET + 1
NG = 4
GE = EX // NG
TOP_G = 2
TOP_K = 4
ROUTE_SCALE = 2.5

W2_PARTS = [("ident", P), ("gate", MT * P), ("up", MT * P), ("down", MT * D), ("router", EX), ("bias", EX),
            ("lower", NG * NG), ("not_first", TJ * EX), ("pick", ET * P)]
W2_COLS, W2_WIDTH = columns(W2_PARTS)


def layer1_experts(nc, ctx, sems, passed, w, loaded, xr, out, NB):

    def sb(name, shape, dtype=F32):
        return ctx.enter_context(nc.sbuf_tensor(name, shape, dtype))

    def pb(name, shape):
        return ctx.enter_context(nc.psum_tensor(name, shape, F32))

    def sem(name):
        return sems.enter_context(nc.semaphore(name))

    signals = {e: [] for e in ("vector", "scalar", "tensor", "gpsimd", "sync")}

    def signal(engine, name, per=1, early=0):
        s = Signal(sem(name), per)
        s.start = LEAD * per - early
        signals[engine].append(s)
        return s

    def prime(eng, engine):
        for s in signals[engine]:
            eng.sem_inc(s.sem, s.start)

    def W(name, *shape):
        a, n = W2_COLS[name]
        v = w[:, a:a + n]
        return v.rearrange("p (a b) -> p a b", a=shape[0]) if len(shape) == 2 else v

    ident = W("ident")
    NTE = PARTS * EX
    pick = sb("pick_b", [NTE, ET, P], BF16)
    ident_b = sb("ident_b", [P, P], BF16)
    st = sb("e_stats", [P, 2, TJ, 6])
    mv = sb("e_mean_var", [P, 2, TJ, 2])
    rs = sb("e_rstd", [P, 2, TJ])
    minus_half = sb("e_minus_half", [P, TJ])
    xn = sb("exp_in", [P, TJ, D])
    xT = sb("exp_in_T", [P, 2, T])
    sc = sb("scores", [P, TJ, EX])
    sfc = sb("biased", [P, TJ, EX])
    top8 = sb("group_top", [P, TJ, NG, 8])
    gs = sb("group_score", [P, TJ, NG])
    above = sb("group_above", [P, TJ, NG, NG])
    equal = sb("group_equal", [P, TJ, NG, NG])
    rank = sb("group_rank", [P, TJ * NG])
    allowed = sb("allowed", [P, TJ, EX])
    best = sb("best", [P, TJ, 8])
    over = sb("over_kth", [P, TJ, EX])
    tied = sb("equal_kth", [P, TJ, EX])
    count = sb("over_count", [P, TJ])
    order = sb("tie_order", [P, TJ, EX])
    wt = sb("route_w", [P, TJ, EX])
    total = sb("route_sum", [P, TJ])
    wp = sb("route_parts", [P, TJ, PARTS, EX], BF16)
    wT = sb("route_parts_T", [NTE, 2, T], BF16)
    RS, RHID = 2, 3
    sg = sb("gated", [P, RS, T])
    hid = sb("hidden", [P, RHID, T])
    dT = sb("mixed_T", [P, T])
    fo = sb("mixed", [P, TJ, D])

    p_g = [pb(f"p_gate{k}", [P, T]) for k in range(2)]
    p_u = [pb(f"p_up{k}", [P, T]) for k in range(2)]
    p_w = [pb(f"p_route{k}", [P, T]) for k in range(2)]
    p_d = pb("p_down", [P, T])
    p_m = pb("p_misc2", [P, T])

    stored = sem("stored")
    set_vec = sem("l2_set_vec")
    set_pe = sem("l2_set_pe")
    SET_VEC = 5
    def hold(eng):
        eng.sem_inc(passed, 1)

    x_stats = signal("vector", "e_x_stats", 2)
    x_rstd = signal("gpsimd", "e_x_rstd", 2)
    x_norm = signal("vector", "e_x_norm")
    x_turned = signal("tensor", "e_x_turned")
    x_copied = signal("scalar", "e_x_copied")
    logits = signal("tensor", "logits")
    scored = signal("scalar", "scored")
    ROUTE = 23
    routed = signal("vector", "routed", ROUTE)
    split_done = signal("vector", "split_done", 2 * (PARTS - 1))
    w_turned = signal("tensor", "w_turned")
    w_copied = signal("scalar", "w_copied")
    gate_ready = signal("tensor", "gate_ready", MT)
    up_ready = signal("tensor", "up_ready", MT)
    w_ready = signal("tensor", "w_ready", ET)
    gated = signal("scalar", "gated", MT)
    upped = signal("vector", "upped", MT)
    weighted = signal("vector", "weighted", ET)
    down_done = signal("tensor", "down_done", MT, 2)
    d_read = signal("scalar", "d_read", 1, 1)
    d_turned = signal("tensor", "d_turned", 1, 1)
    fo_read = signal("scalar", "e_fo_read", 1, 1)
    fo_stats = signal("vector", "e_fo_stats", 2, 2)
    fo_rstd = signal("gpsimd", "e_fo_rstd", 2, 2)
    fo_norm = signal("vector", "e_fo_norm", 1, 1)
    added = signal("vector", "e_added", 1, 1)

    def X(s):
        return xr[:, bass.ds((s + FRONT) * TJ, TJ), :]

    def Xj(s, j):
        return xr[:, bass.ds((s + FRONT) * TJ + j, 1), :].rearrange("p a d -> p (a d)")

    block = ctx.enter_context(nc.Block())

    @block.sync
    def _(sp):
        for s in range(NB):
            sp.wait_ge(added.sem, added.at(s))
            sp.dma_start(out[s].rearrange("(j p) d -> p j d", p=P),
                         xr[:, TJ * (s + FRONT):TJ * (s + FRONT + 1), :]).then_inc(stored, 16)
        sp.wait_ge(stored, 16 * NB)

    @block.tensor
    def _(pe):
        prime(pe, "tensor")
        pe.wait_ge(loaded, 16)
        pe.wait_ge(set_vec, SET_VEC)
        nc.tensor.matmul(p_d[:, :], ident, hid[:, 0, :], start=True, stop=False).then_inc(set_pe, 1)

        def x_turn(s):
            pe.wait_ge(x_norm.sem, x_norm.at(s))
            pe.wait_ge(w_copied.sem, w_copied.at(s - 1))
            for j in range(TJ):
                last = nc.tensor.transpose(p_m[:, j * P:(j + 1) * P], xn[:, j, :], ident)
            last.then_inc(x_turned.sem, 1)

        def route(s, b):
            pe.wait_ge(x_copied.sem, x_copied.at(s))
            for j in range(TJ):
                last = nc.tensor.matmul(p_m[:, j * EX:(j + 1) * EX], xT[:, b, j * P:(j + 1) * P], W("router"),
                                        start=True, stop=True)
            last.then_inc(logits.sem, 1)

        def w_turn(s):
            pe.wait_ge(routed.sem, routed.at(s))
            pe.wait_ge(scored.sem, scored.at(s))
            pe.wait_ge(fo_read.sem, fo_read.at(s - 2))
            for j in range(TJ):
                last = nc.tensor.matmul(p_m[0:NTE, j * P:(j + 1) * P],
                                        wp[:, j, :, :].rearrange("p k e -> p (k e)"), ident_b[:, :],
                                        start=True, stop=True)
            last.then_inc(w_turned.sem, 1)

        def gate_up(s, b, n):
            k = (n + b) % 2
            pe.wait_ge(gated.sem, gated.at(s, n - 1))
            nc.tensor.matmul(p_g[k][:, :], W("gate", MT, P)[:, n, :], xT[:, b, :], start=True, stop=True)\
                .then_inc(gate_ready.sem, 1)
            pe.wait_ge(upped.sem, upped.at(s, n - 1))
            nc.tensor.matmul(p_u[k][:, :], W("up", MT, P)[:, n, :], xT[:, b, :], start=True, stop=True)\
                .then_inc(up_ready.sem, 1)

        def spread_w(s, b, n):
            if n == 0:
                pe.wait_ge(w_copied.sem, w_copied.at(s))
            pe.wait_ge(weighted.sem, weighted.at(s, n - 1))
            nc.tensor.matmul(p_w[n % 2][:, :], pick[:, n, :], wT[:, b, :], start=True, stop=True)\
                .then_inc(w_ready.sem, 1)

        def down(s, n):
            if n == 0:
                pe.wait_ge(d_read.sem, d_read.at(s - 1))
            if n < ET:
                pe.wait_ge(weighted.sem, weighted.at(s, n + 1))
            else:
                pe.wait_ge(upped.sem, upped.at(s))
            nc.tensor.matmul(p_d[:, :], W("down", MT, D)[:, n, :], hid[:, n % RHID, :],
                             start=(n == 0), stop=(n == MT - 1)).then_inc(down_done.sem, 1)

        def turn_mixed(s, last_step):
            pe.wait_ge(d_read.sem, d_read.at(s))
            if not last_step:
                pe.wait_ge(scored.sem, scored.at(s + 2))
            for j in range(TJ):
                last = nc.tensor.transpose(p_m[:, j * P:(j + 1) * P], dT[:, j * P:(j + 1) * P], ident)
            last.then_inc(d_turned.sem, 1)

        def prepare(s, b, n):
            if n == 3:
                x_turn(s)
            if n == 4:
                route(s, b)
            if n == 12:
                w_turn(s)

        def finish(s, n, last_step=False):
            if n < 2:
                down(s, MT - 2 + n)
            if n == 5:
                turn_mixed(s, last_step)

        for n in range(MT):
            prepare(0, 0, n)
        with pe.Fori(0, NB // 2) as m:
            for b in range(2):
                s = 2 * m + b
                for n in range(MT):
                    gate_up(s, b, n)
                    if n < ET:
                        spread_w(s, b, n)
                    if n >= 2:
                        down(s, n - 2)
                    prepare(s + 1, 1 - b, n)
                    finish(s - 1, n)
        for n in range(MT):
            finish(NB - 1, n, last_step=True)

    @block.scalar
    def _(act):
        prime(act, "scalar")
        act.wait_ge(set_vec, SET_VEC)
        act.wait_ge(set_pe, 1)

        def x_copy(s, b):
            act.wait_ge(x_turned.sem, x_turned.at(s))
            act.wait_ge(up_ready.sem, up_ready.at(s - 2))
            nc.scalar.activation(xT[:, b, :], p_m[:, :], ACT.Copy).then_inc(x_copied.sem, 1)

        def score(s):
            act.wait_ge(logits.sem, logits.at(s))
            act.wait_ge(routed.sem, routed.at(s - 1))
            nc.scalar.activation(sc[:, :, :], p_m[:, 0:TJ * EX].rearrange("p (j e) -> p j e", j=TJ), ACT.Sigmoid)\
                .then_inc(scored.sem, 1)

        def w_copy(s, b):
            act.wait_ge(w_turned.sem, w_turned.at(s))
            act.wait_ge(w_ready.sem, w_ready.at(s - 2))
            nc.scalar.activation(wT[:, b, :], p_m[0:NTE, :], ACT.Copy).then_inc(w_copied.sem, 1)

        def silu(s, b, n):
            k = (n + b) % 2
            act.wait_ge(gate_ready.sem, gate_ready.at(s, n + 1))
            act.wait_ge(upped.sem, upped.at(s, n - 1))
            nc.scalar.activation(sg[:, k, :], p_g[k][:, :], ACT.Silu).then_inc(gated.sem, 1)

        def copy_down(s):
            act.wait_ge(down_done.sem, down_done.at(s))
            act.wait_ge(d_turned.sem, d_turned.at(s - 1))
            nc.scalar.activation(dT[:, :], p_d[:, :], ACT.Copy).then_inc(d_read.sem, 1)

        def copy_mixed(s):
            act.wait_ge(d_turned.sem, d_turned.at(s))
            act.wait_ge(added.sem, added.at(s - 1))
            nc.scalar.activation(fo[:, :, :], p_m[:, :].rearrange("p (j d) -> p j d", j=TJ), ACT.Copy)\
                .then_inc(fo_read.sem, 1)

        def prepare(s, b, n):
            if n == 3:
                x_copy(s, b)
            if n == 4:
                score(s)
            if n == 12:
                w_copy(s, b)

        def finish(s, n):
            if n == 1:
                copy_down(s)
            if n == 5:
                copy_mixed(s)

        for n in range(MT):
            prepare(0, 0, n)
        with act.Fori(0, NB // 2) as m:
            for b in range(2):
                s = 2 * m + b
                for n in range(MT):
                    silu(s, b, n)
                    prepare(s + 1, 1 - b, n)
                    finish(s - 1, n)
        for n in range(MT):
            finish(NB - 1, n)

    @block.vector
    def _(dve):
        prime(dve, "vector")
        nc.vector.memset(hid[:, :, :], 0.0).then_inc(set_vec, 1)
        nc.vector.memset(minus_half[:, :], -0.5).then_inc(set_vec, 1)
        dve.wait_ge(loaded, 16)
        nc.vector.tensor_copy(pick[:, :, :], W("pick", ET, P)[0:NTE, :, :]).then_inc(set_vec, 1)
        nc.vector.tensor_copy(ident_b[:, :], ident).then_inc(set_vec, 1)
        nc.vector.memset(total[:, :], 0.0).then_inc(set_vec, 1)
        dve.wait_ge(set_vec, SET_VEC)
        dve.wait_ge(set_pe, 1)

        def stats(s, at, src, done):
            hold(dve)
            for j in range(TJ):
                last = nc.vector.bn_stats(st[:, at, j, :], src(j))
            last.then_inc(done.sem, 1)
            dve.wait_ge(done.sem, done.at(s, 1))
            hold(dve)
            for j in range(TJ):
                last = nc.vector.bn_aggr(mv[:, at, j, :], st[:, at, j, :])
            last.then_inc(done.sem, 1)

        def normalize(dst, src, at):
            for j in range(TJ):
                last = nc.vector.tensor_scalar(dst(j), src(j), mv[:, at, j, 0:1], rs[:, at, j:j + 1],
                                               ALU.subtract, ALU.mult)
            return last

        def x_stat(s):
            dve.wait_ge(x_norm.sem, x_norm.at(s - 1))
            stats(s, 0, lambda j: Xj(s, j), x_stats)

        def x_normalize(s):
            dve.wait_ge(x_rstd.sem, x_rstd.at(s))
            dve.wait_ge(x_turned.sem, x_turned.at(s - 1))
            normalize(lambda j: xn[:, j, :], lambda j: Xj(s, j), 0).then_inc(x_norm.sem, 1)

        def each(a, n):
            return a.unsqueeze(len(a.shape)).broadcast_to(list(a.shape) + [n])

        def group_scores(s):
            dve.wait_ge(scored.sem, scored.at(s))
            dve.wait_ge(routed.sem, routed.at(s, 0))
            nc.vector.tensor_tensor(sfc[:, :, :], sc[:, :, :],
                                    W("bias").unsqueeze(1).broadcast_to([P, TJ, EX]), ALU.add)\
                .then_inc(routed.sem, 1)
            dve.wait_ge(routed.sem, routed.at(s, 1))
            hold(dve)
            for j in range(TJ):
                for g in range(NG):
                    last = nc.vector.max(top8[:, j, g, :], sfc[:, j, g * GE:(g + 1) * GE])
            last.then_inc(routed.sem, 1)
            dve.wait_ge(routed.sem, routed.at(s, 2))
            nc.vector.tensor_tensor(gs[:, :, :], top8[:, :, :, 0], top8[:, :, :, 1], ALU.add)\
                .then_inc(routed.sem, 1)

        def group_ranks(s):
            dve.wait_ge(routed.sem, routed.at(s, 3))
            other = gs[:, :, :].unsqueeze(2).broadcast_to([P, TJ, NG, NG])
            own = each(gs[:, :, :], NG)
            nc.vector.tensor_tensor(above[:, :, :, :], other, own, ALU.is_gt).then_inc(routed.sem, 1)
            nc.vector.tensor_tensor(equal[:, :, :, :], other, own, ALU.is_equal).then_inc(routed.sem, 1)
            dve.wait_ge(routed.sem, routed.at(s, 5))
            lower = W("lower", NG, NG).unsqueeze(1).broadcast_to([P, TJ, NG, NG])
            nc.vector.tensor_tensor(equal[:, :, :, :], equal[:, :, :, :], lower, ALU.mult).then_inc(routed.sem, 1)
            dve.wait_ge(routed.sem, routed.at(s, 6))
            nc.vector.tensor_tensor(above[:, :, :, :], above[:, :, :, :], equal[:, :, :, :], ALU.add)\
                .then_inc(routed.sem, 1)
            dve.wait_ge(routed.sem, routed.at(s, 7))
            nc.vector.tensor_reduce(rank[:, :], above[:, :, :, :].rearrange("p j g h -> p (j g) h"), AX.X, ALU.add)\
                .then_inc(routed.sem, 1)

        def kth_best(s):
            dve.wait_ge(routed.sem, routed.at(s, 8))
            nc.vector.scalar_tensor_tensor(out=allowed[:, :, :].rearrange("p j (g e) -> p (j g) e", g=NG),
                                           in0=each(rank[:, :], GE), scalar=float(TOP_G),
                                           in1=sfc[:, :, :].rearrange("p j (g e) -> p (j g) e", g=NG),
                                           op0=ALU.is_lt, op1=ALU.mult).then_inc(routed.sem, 1)
            dve.wait_ge(routed.sem, routed.at(s, 9))
            hold(dve)
            for j in range(TJ):
                last = nc.vector.max(best[:, j, :], allowed[:, j, :])
            last.then_inc(routed.sem, 1)

        def choose(s):
            dve.wait_ge(routed.sem, routed.at(s, 10))
            kth = best[:, :, TOP_K - 1:TOP_K].broadcast_to([P, TJ, EX])
            nc.vector.tensor_tensor(over[:, :, :], allowed[:, :, :], kth, ALU.is_gt).then_inc(routed.sem, 1)
            nc.vector.tensor_tensor(tied[:, :, :], allowed[:, :, :], kth, ALU.is_equal).then_inc(routed.sem, 1)
            dve.wait_ge(routed.sem, routed.at(s, 12))
            nc.vector.tensor_reduce(count[:, :], over[:, :, :], AX.X, ALU.add).then_inc(routed.sem, 1)
            nc.vector.tensor_tensor_scan(order[:, :, :].rearrange("p j e -> p (j e)"), W("not_first"),
                                         tied[:, :, :].rearrange("p j e -> p (j e)"), 0.0, ALU.mult, ALU.add)\
                .then_inc(routed.sem, 1)
            dve.wait_ge(routed.sem, routed.at(s, 14))
            nc.vector.tensor_tensor(order[:, :, :], order[:, :, :], each(count[:, :], EX), ALU.add)\
                .then_inc(routed.sem, 1)
            dve.wait_ge(routed.sem, routed.at(s, 15))
            nc.vector.scalar_tensor_tensor(out=tied[:, :, :], in0=order[:, :, :], scalar=float(TOP_K),
                                           in1=tied[:, :, :], op0=ALU.is_le, op1=ALU.mult).then_inc(routed.sem, 1)
            dve.wait_ge(routed.sem, routed.at(s, 16))
            nc.vector.tensor_tensor(over[:, :, :], over[:, :, :], tied[:, :, :], ALU.add).then_inc(routed.sem, 1)

        def weights(s):
            dve.wait_ge(routed.sem, routed.at(s, 17))
            nc.vector.tensor_tensor(wt[:, :, :], sc[:, :, :], over[:, :, :], ALU.mult).then_inc(routed.sem, 1)
            dve.wait_ge(routed.sem, routed.at(s, 18))
            nc.vector.tensor_reduce(total[:, :], wt[:, :, :], AX.X, ALU.add).then_inc(routed.sem, 1)
            dve.wait_ge(routed.sem, routed.at(s, 19))
            nc.vector.tensor_scalar(total[:, :], total[:, :], 1e-20, None, ALU.add).then_inc(routed.sem, 1)
            dve.wait_ge(routed.sem, routed.at(s, 20))
            nc.vector.reciprocal(total[:, :], total[:, :]).then_inc(routed.sem, 1)
            dve.wait_ge(routed.sem, routed.at(s, 21))
            nc.vector.scalar_tensor_tensor(out=wt[:, :, :], in0=wt[:, :, :], scalar=ROUTE_SCALE,
                                           in1=each(total[:, :], EX), op0=ALU.mult, op1=ALU.mult)\
                .then_inc(routed.sem, 1)

        def split(s):
            for k in range(PARTS):
                dve.wait_ge(split_done.sem, split_done.at(s, 2 * k))
                if k == 0:
                    dve.wait_ge(routed.sem, routed.at(s, 22))
                    dve.wait_ge(w_turned.sem, w_turned.at(s - 1))
                if k == PARTS - 1:
                    nc.vector.tensor_copy(wp[:, :, k, :], wt[:, :, :]).then_inc(routed.sem, 1)
                    continue
                nc.vector.tensor_copy(wp[:, :, k, :], wt[:, :, :]).then_inc(split_done.sem, 1)
                dve.wait_ge(split_done.sem, split_done.at(s, 2 * k + 1))
                nc.vector.tensor_tensor(wt[:, :, :], wt[:, :, :], wp[:, :, k, :], ALU.subtract)\
                    .then_inc(split_done.sem, 1)

        def multiply_up(s, b, n):
            k = (n + b) % 2
            dve.wait_ge(up_ready.sem, up_ready.at(s, n + 1))
            dve.wait_ge(gated.sem, gated.at(s, n + 1))
            dve.wait_ge(down_done.sem, down_done.at(s, n - 2) if n >= RHID else
                        down_done.at(s - 1, MT - 1 if n == 0 else MT))
            nc.vector.tensor_tensor(hid[:, n % RHID, :], p_u[k][:, :], sg[:, k, :], ALU.mult)\
                .then_inc(upped.sem, 1)

        def weigh(s, n):
            dve.wait_ge(upped.sem, upped.at(s, n + 1))
            dve.wait_ge(w_ready.sem, w_ready.at(s, n + 1))
            nc.vector.tensor_tensor(hid[:, n % RHID, :], hid[:, n % RHID, :], p_w[n % 2][:, :], ALU.mult)\
                .then_inc(weighted.sem, 1)

        def out_stats(s):
            dve.wait_ge(fo_read.sem, fo_read.at(s))
            dve.wait_ge(fo_norm.sem, fo_norm.at(s - 1))
            stats(s, 1, lambda j: fo[:, j, :], fo_stats)

        def add(s):
            dve.wait_ge(fo_rstd.sem, fo_rstd.at(s))
            normalize(lambda j: fo[:, j, :], lambda j: fo[:, j, :], 1).then_inc(fo_norm.sem, 1)
            dve.wait_ge(fo_norm.sem, fo_norm.at(s))
            nc.vector.tensor_tensor(X(s), X(s), fo[:, :, :], ALU.add).then_inc(added.sem, 1)

        def prepare(s, n):
            if n == 0:
                x_stat(s)
            if n == 2:
                x_normalize(s)
            if n == 5:
                group_scores(s)
            if n == 6:
                group_ranks(s)
            if n == 7:
                kth_best(s)
            if n == 8:
                choose(s)
            if n == 9:
                weights(s)
            if n == 10:
                split(s)

        def finish(s, n):
            if n == 11:
                out_stats(s)
            if n == 13:
                add(s)

        for n in range(MT):
            prepare(0, n)
        with dve.Fori(0, NB // 2) as m:
            for b in range(2):
                s = 2 * m + b
                for n in range(MT):
                    multiply_up(s, b, n)
                    if n < ET:
                        weigh(s, n)
                    prepare(s + 1, n)
                    finish(s - 1, n)
        for n in range(MT):
            finish(NB - 1, n)

    @block.gpsimd
    def _(pool):
        prime(pool, "gpsimd")
        pool.wait_ge(set_vec, SET_VEC)

        def rstd(s, at, stats, done):
            pool.wait_ge(stats.sem, stats.at(s))
            hold(pool)
            nc.gpsimd.tensor_scalar(rs[:, at, :], mv[:, at, :, 1], LN_EPS, None, ALU.add).then_inc(done.sem, 1)
            pool.wait_ge(done.sem, done.at(s, 1))
            nc.gpsimd.tensor_tensor(rs[:, at, :], rs[:, at, :], minus_half[:, :], ALU.pow).then_inc(done.sem, 1)

        rstd(0, 0, x_stats, x_rstd)
        with pool.Fori(0, NB) as s:
            rstd(s + 1, 0, x_stats, x_rstd)
            rstd(s - 1, 1, fo_stats, fo_rstd)
        rstd(NB - 1, 1, fo_stats, fo_rstd)


def pack_experts(i):
    q = np.arange(P)
    shared = lambda a: np.asarray(a, np.float32)
    gate = np.concatenate([i["L1_ffn_gate_w"].reshape(EX * EH, D), shared(i["L1_ffn_shared_gate_w"])])
    up = np.concatenate([i["L1_ffn_up_w"].reshape(EX * EH, D), shared(i["L1_ffn_shared_up_w"])])
    down = np.concatenate([i["L1_ffn_down_w"].transpose(0, 2, 1).reshape(EX * EH, D),
                           shared(i["L1_ffn_shared_down_w"]).T])
    pick = np.zeros((P, ET, P), np.float32)
    for n in range(ET):
        pick[:PARTS * EX, n, :] = (np.arange(PARTS * EX) % EX)[:, None] == PAIR * n + q[None, :] // EH
    g = np.arange(NG)
    return pack(W2_PARTS, W2_WIDTH, {
        "ident": np.eye(P, dtype=np.float32),
        "gate": gate.T, "up": up.T, "down": rows_first(down),
        "router": i["L1_ffn_router_weight"].T,
        "bias": np.broadcast_to(i["L1_ffn_router_bias"][None, :], (P, EX)),
        "lower": np.broadcast_to((g[None, :] < g[:, None]).reshape(1, -1), (P, NG * NG)),
        "not_first": np.broadcast_to((np.arange(TJ * EX) % EX != 0)[None, :], (P, TJ * EX)),
        "pick": pick,
    })


B = 16


def sandwich_kernel(nc, x_in, w0_in, s0_in, w1_in, w2_in, out):
    scratch = nc.dram_tensor("q_k_scratch", (2, 2, PARTS, P, T), BF16).ap()
    with ExitStack() as whole:
        passed = whole.enter_context(nc.semaphore("passed"))
        xr = whole.enter_context(nc.sbuf_tensor("residual", [P, TJ * (FRONT + B + 2), D], F32))
        with ExitStack() as ctx:
            layer0(nc, ctx, whole, passed, x_in, w0_in, s0_in, xr, None, B)
        w2 = whole.enter_context(nc.sbuf_tensor("w2", [P, W2_WIDTH], F32))
        w2_loaded = whole.enter_context(nc.semaphore("w2_loaded"))
        with ExitStack() as ctx:
            layer1_attention(nc, ctx, whole, passed, w2, w2_loaded, w2_in, w1_in, scratch, xr, None, B)
        with ExitStack() as ctx:
            layer1_experts(nc, ctx, whole, passed, w2, w2_loaded, xr, out, B)


def kernel(**inputs):
    import concourse.bacc as _bacc
    from concourse.bass_utils import run_bass_kernel_spmd as _run

    i = {name: np.asarray(a) for name, a in inputs.items()}
    w0, s0 = pack_layer0(i)
    arrays = {"x_in": np.ascontiguousarray(i["L0_attn_x"]), "w0_in": w0, "s0_in": s0,
              "w1_in": pack_layer1(i), "w2_in": pack_experts(i)}
    nc = _bacc.Bacc("TRN2", target_bir_lowering=False, num_devices=1)
    args = [nc.dram_tensor(name, a.shape, mybir.dt.from_np(a.dtype), kind="ExternalInput").ap()
            for name, a in arrays.items()]
    out = nc.dram_tensor("out", (B, T, D), F32, kind="ExternalOutput").ap()
    sandwich_kernel(nc, *args, out)
    r = _run(nc, [arrays], core_ids=[0])
    return r.results[0]["out"]
```
